# Optimizing a Trainium2 kernel written in Bass

```python
import numpy as np
import jax
import jax.numpy as jnp

def _softmax(x, axis=-1):
    return jax.nn.softmax(x, axis=axis)

def _gelu(x):
    return jax.nn.gelu(x, approximate=True)

def _silu(x):
    return jax.nn.silu(x)

def _sigmoid(x):
    return jax.nn.sigmoid(x)

def _layernorm(x, axis=-1, eps=1e-05):
    m = jnp.mean(x, axis=axis, keepdims=True)
    v = jnp.var(x, axis=axis, keepdims=True)
    return (x - m) / jnp.sqrt(v + eps)

def _scatter_add(tgt, idx, src, axis=0):
    return tgt.at[idx].add(src)

def _segment_sum(src, seg, n):
    return jax.ops.segment_sum(src, seg, n)
kernel_name = 'mk_decoder_preln_d1_seqx_r8_32edfe'

def setup_inputs(seed: int=0):
    np.random.seed(seed)
    _w = jnp.asarray

    def _rec_inputs():
        import jax
        import jax.numpy as jnp
        _rk = jax.random.key(seed)
        x = 7.22e-05 + 1 * jax.random.normal(jax.random.fold_in(_rk, 1), (64, 64, 128), jnp.float32)
        _lenS = 64 - jax.random.randint(jax.random.fold_in(_rk, 7), (64,), 0, max(1, 64 // 4) + 1, jnp.int32)
        _lenS2 = 64 - jax.random.randint(jax.random.fold_in(_rk, 8), (64,), 0, max(1, 64 // 4) + 1, jnp.int32)
        _ctx_1024P = jax.random.normal(jax.random.fold_in(_rk, 11), (64, 16, 128), jnp.float32)
        _ctx_1024c = jax.random.dirichlet(jax.random.fold_in(_rk, 511), 0.3 * jnp.ones((16,), jnp.float32), (64, 64))
        _ctx_1024t = jnp.einsum('bsk,bkd->bsd', _ctx_1024c, _ctx_1024P)
        _ctx_1024t = _ctx_1024t * jax.lax.rsqrt(jnp.mean(jnp.square(_ctx_1024t)) + 1e-12) * 0.953939
        ctx_1024 = 4.13588e-05 + 0.999923 * (_ctx_1024t + 0.3 * jax.random.normal(jax.random.fold_in(_rk, 611), (64, 64, 128), jnp.float32))
        _validS = jnp.arange(64)[None, :] < _lenS[:, None]
        _validS2 = jnp.arange(64)[None, :] < _lenS2[:, None]
        _causal = jnp.tril(jnp.ones((64, 64), dtype=bool))
        mask_BxS2_bk0 = jnp.logical_not(jnp.broadcast_to(_validS2[:, :], (64, 64)))
        return (x, ctx_1024, mask_BxS2_bk0)
    x, ctx_1024, mask_BxS2_bk0 = _rec_inputs()

    def _L0_attn_setup():
        import jax, jax.numpy as jnp
        import numpy as np
        B, S, E, H = (2, 256, 128, 16)
        D = E // H
        TRIL = D * (D + 1) // 2
        key = jax.random.key(seed)
        ks = jax.random.split(key, 6)
        return {'x': jax.random.normal(ks[0], (B, S, E), dtype=jnp.float32), 'params': jax.random.normal(ks[1], (H, TRIL), dtype=jnp.float32), 'Wv': jax.random.normal(ks[2], (E, E), dtype=jnp.float32) * 0.02, 'bv': jax.random.normal(ks[3], (E,), dtype=jnp.float32) * 0.02, 'Wo': jax.random.normal(ks[4], (E, E), dtype=jnp.float32) * 0.02, 'bo': jax.random.normal(ks[5], (E,), dtype=jnp.float32) * 0.02}
    _L0_attn_all = _L0_attn_setup()
    _L0_attn_in = {k: v for k, v in _L0_attn_all.items() if k in ('params', 'Wv', 'bv', 'Wo', 'bo')}
    del _L0_attn_all

    def _L0_xattn_setup():
        import jax, jax.numpy as jnp
        import numpy as np
        NUM_HEADS = 16
        HIDDEN = 128
        KEY_SIZE = 64
        VALUE_SIZE = 64
        B, S = (4, 256)

        def _split_heads(x, d):
            b, s, _ = x.shape
            return x.reshape(b, s, NUM_HEADS, d).transpose(0, 2, 1, 3)
        key = jax.random.key(seed)
        ks = jax.random.split(key, 7)
        xavier = lambda k, shp: jax.random.normal(k, shp, jnp.float32) * jnp.sqrt(2.0 / (shp[0] + shp[1]))
        return {'X_Q': jax.random.normal(ks[0], (B, S, HIDDEN), jnp.float32), 'X_KV': jax.random.normal(ks[1], (B, S, HIDDEN), jnp.float32), 'key_padding_mask': jax.random.randint(ks[2], (B, S), 0, 2).astype(bool), 'W_Q': xavier(ks[3], (HIDDEN, KEY_SIZE * NUM_HEADS)), 'W_K': xavier(ks[4], (HIDDEN, KEY_SIZE * NUM_HEADS)), 'W_V': xavier(ks[5], (HIDDEN, VALUE_SIZE * NUM_HEADS)), 'W_O': xavier(ks[6], (VALUE_SIZE * NUM_HEADS, HIDDEN))}
    _L0_xattn_all = _L0_xattn_setup()
    _L0_xattn_in = {k: v for k, v in _L0_xattn_all.items() if k in ('W_Q', 'W_K', 'W_V', 'W_O')}
    del _L0_xattn_all

    def _L0_ffn_setup():
        import jax, jax.numpy as jnp
        import numpy as np
        DIM = 128
        DEPTH = 6
        HEADS = 16
        DIM_HEAD = 64
        WINDOW = 32
        INNER = HEADS * DIM_HEAD
        DIM_INNER = int(DIM * 4 * 2 / 3)
        QK_SCALE = 8.0

        def shift_tokens(t):
            a, s = jnp.split(t, 2, -1)
            s = jnp.pad(s, ((0, 0), (1, 0), (0, 0)))[:, :-1]
            return jnp.concatenate([a, s], -1)

        def l2norm(t):
            return t / jnp.maximum(jnp.linalg.norm(t, axis=-1, keepdims=True), 1e-12)

        def rotate_half(x):
            x1, x2 = jnp.split(x, 2, -1)
            return jnp.concatenate([-x2, x1], -1)

        def rotary_tables(n):
            half = jnp.arange(0, DIM_HEAD, 2, dtype=jnp.float32)
            inv_freq = 1.0 / 10000.0 ** (half / DIM_HEAD)
            t = jnp.arange(n, dtype=jnp.float32)
            freqs = t[:, None] * inv_freq[None, :]
            freqs = jnp.concatenate([freqs, freqs], -1)
            base_scale = (half + 0.4 * DIM_HEAD) / (1.4 * DIM_HEAD)
            power = (t - n // 2) / (WINDOW // 2)
            scale = base_scale[None, :] ** power[:, None]
            scale = jnp.concatenate([scale, scale], -1)
            return (freqs, scale)

        def local_attention(q, k, v):
            b, h, n, d = q.shape
            w = WINDOW
            nw = n // w
            bq = q.reshape(b, h, nw, w, d)
            bk = k.reshape(b, h, nw, w, d)
            bv = v.reshape(b, h, nw, w, d)

            def look(t):
                p = jnp.pad(t, ((0, 0), (0, 0), (1, 0), (0, 0), (0, 0)))
                return jnp.concatenate([p[:, :, :nw], p[:, :, 1:]], axis=3)
            bk2, bv2 = (look(bk), look(bv))
            seq = jnp.arange(n).reshape(nw, w)
            seq_p = jnp.pad(seq, ((1, 0), (0, 0)), constant_values=-1)
            jt = jnp.concatenate([seq_p[:nw], seq_p[1:]], axis=1)
            it = seq[:, :, None]
            jb = jt[:, None, :]
            mask = (it < jb) | (it > jb + w) | (jb == -1)
            sim = jnp.einsum('bhwie,bhwje->bhwij', bq, bk2) * QK_SCALE
            sim = jnp.where(mask, -jnp.finfo(sim.dtype).max, sim)
            attn = jax.nn.softmax(sim, -1)
            out = jnp.einsum('bhwij,bhwje->bhwie', attn, bv2)
            return out.reshape(b, h, n, d)

        def attn_layer(x, Wqkv, qs, ksc, Wo):
            b, n, _ = x.shape
            qkv = x @ Wqkv
            q, k, v = jnp.split(qkv, 3, -1)
            sh = lambda t: t.reshape(b, n, HEADS, DIM_HEAD).transpose(0, 2, 1, 3)
            q, k, v = (sh(q), sh(k), sh(v))
            q = l2norm(q) * qs
            k = l2norm(k) * ksc
            freqs, scale = rotary_tables(n)
            cos, sin = (jnp.cos(freqs), jnp.sin(freqs))
            q = q * cos * scale + rotate_half(q) * sin * scale
            inv = 1.0 / scale
            k = k * cos * inv + rotate_half(k) * sin * inv
            out = local_attention(q, k, v)
            out = out.transpose(0, 2, 1, 3).reshape(b, n, INNER)
            return out @ Wo

        def ffn_layer(x, g, bln, W1, b1, W2, b2):
            mu = x.mean(-1, keepdims=True)
            var = ((x - mu) ** 2).mean(-1, keepdims=True)
            xn = (x - mu) / jnp.sqrt(var + 1e-05) * g + bln
            hg = xn @ W1 + b1
            a, gate = jnp.split(hg, 2, -1)
            return a * jax.nn.gelu(gate, approximate=False) @ W2 + b2
        key = jax.random.key(seed)
        ks = jax.random.split(key, 8)
        B, N = (2, 256)
        init = lambda k, shape: jax.random.normal(k, shape, jnp.float32) * 0.02
        return {'x': jax.random.normal(ks[0], (B, N, DIM), jnp.float32), 'Wqkv': init(ks[1], (DEPTH, DIM, 3 * INNER)), 'q_scale': jnp.ones((DEPTH, DIM_HEAD), jnp.float32), 'k_scale': jnp.ones((DEPTH, DIM_HEAD), jnp.float32), 'Wo': init(ks[2], (DEPTH, INNER, DIM)), 'ln_g': jnp.ones((DEPTH, DIM), jnp.float32), 'ln_b': jnp.zeros((DEPTH, DIM), jnp.float32), 'W1': init(ks[3], (DEPTH, DIM, 2 * DIM_INNER)), 'b1': jnp.zeros((DEPTH, 2 * DIM_INNER), jnp.float32), 'W2': init(ks[4], (DEPTH, DIM_INNER, DIM)), 'b2': jnp.zeros((DEPTH, DIM), jnp.float32)}
    _L0_ffn_all = _L0_ffn_setup()
    _L0_ffn_in = {k: v for k, v in _L0_ffn_all.items() if k in ('Wqkv', 'q_scale', 'k_scale', 'Wo', 'ln_g', 'ln_b', 'W1', 'b1', 'W2', 'b2')}
    del _L0_ffn_all
    return {'x': x, 'ctx_1024': ctx_1024, 'mask_BxS2_bk0': mask_BxS2_bk0, 'L0_attn_params': _L0_attn_in['params'], 'L0_attn_Wv': _L0_attn_in['Wv'], 'L0_attn_bv': _L0_attn_in['bv'], 'L0_attn_Wo': _L0_attn_in['Wo'], 'L0_attn_bo': _L0_attn_in['bo'], 'L0_xattn_W_Q': _L0_xattn_in['W_Q'], 'L0_xattn_W_K': _L0_xattn_in['W_K'], 'L0_xattn_W_V': _L0_xattn_in['W_V'], 'L0_xattn_W_O': _L0_xattn_in['W_O'], 'L0_ffn_Wqkv': _L0_ffn_in['Wqkv'], 'L0_ffn_q_scale': _L0_ffn_in['q_scale'], 'L0_ffn_k_scale': _L0_ffn_in['k_scale'], 'L0_ffn_Wo': _L0_ffn_in['Wo'], 'L0_ffn_ln_g': _L0_ffn_in['ln_g'], 'L0_ffn_ln_b': _L0_ffn_in['ln_b'], 'L0_ffn_W1': _L0_ffn_in['W1'], 'L0_ffn_b1': _L0_ffn_in['b1'], 'L0_ffn_W2': _L0_ffn_in['W2'], 'L0_ffn_b2': _L0_ffn_in['b2']}

def reference(x, ctx_1024, mask_BxS2_bk0, L0_attn_params, L0_attn_Wv, L0_attn_bv, L0_attn_Wo, L0_attn_bo, L0_xattn_W_Q, L0_xattn_W_K, L0_xattn_W_V, L0_xattn_W_O, L0_ffn_Wqkv, L0_ffn_q_scale, L0_ffn_k_scale, L0_ffn_Wo, L0_ffn_ln_g, L0_ffn_ln_b, L0_ffn_W1, L0_ffn_b1, L0_ffn_W2, L0_ffn_b2):
    import jax
    import jax.numpy as jnp

    def _L0_attn_ref(x, params, Wv, bv, Wo, bo):
        import jax, jax.numpy as jnp
        import numpy as np
        B, S, E, H = (2, 256, 128, 16)
        D = E // H
        TRIL = D * (D + 1) // 2
        bs, seq_len, emb_dim = x.shape
        d = D
        rows, cols = jnp.tril_indices(d)
        tril = jnp.zeros((H, d, d), dtype=x.dtype).at[:, rows, cols].set(params)
        Wqk = jnp.einsum('hij,hkj->hik', tril, tril)
        xh = x.reshape(bs, seq_len, H, d)
        t = jnp.einsum('bshd,hde->bshe', xh, Wqk)
        scores = jnp.einsum('bshe,bthe->bhst', t, xh) / jnp.sqrt(jnp.asarray(d, x.dtype))
        attn = jax.nn.softmax(scores, axis=-1)
        Vh = (x @ Wv.T + bv).reshape(bs, seq_len, H, d)
        out = jnp.einsum('bhst,bthd->bshd', attn, Vh).reshape(bs, seq_len, emb_dim)
        return out @ Wo.T + bo

    def _L0_xattn_ref(X_Q, X_KV, key_padding_mask, W_Q, W_K, W_V, W_O):
        import jax, jax.numpy as jnp
        import numpy as np
        NUM_HEADS = 16
        HIDDEN = 128
        KEY_SIZE = 64
        VALUE_SIZE = 64
        B, S = (4, 256)

        def _split_heads(x, d):
            b, s, _ = x.shape
            return x.reshape(b, s, NUM_HEADS, d).transpose(0, 2, 1, 3)
        Q = _split_heads(X_Q @ W_Q, KEY_SIZE)
        K = _split_heads(X_KV @ W_K, KEY_SIZE)
        V = _split_heads(X_KV @ W_V, VALUE_SIZE)
        E = jnp.einsum('bhqd,bhkd->bhqk', Q, K)
        E = jnp.where(key_padding_mask[:, None, None, :], -jnp.inf, E)
        A = jax.nn.softmax(E / jnp.sqrt(jnp.float32(KEY_SIZE)), axis=-1)
        Yp = jnp.einsum('bhqk,bhkd->bhqd', A, V)
        b, h, sq, dv = Yp.shape
        Y = Yp.transpose(0, 2, 1, 3).reshape(b, sq, h * dv) @ W_O
        return Y

    def _L0_ffn_ref(x, Wqkv, q_scale, k_scale, Wo, ln_g, ln_b, W1, b1, W2, b2):
        import jax, jax.numpy as jnp
        import numpy as np
        DIM = 128
        DEPTH = 6
        HEADS = 16
        DIM_HEAD = 64
        WINDOW = 32
        INNER = HEADS * DIM_HEAD
        DIM_INNER = int(DIM * 4 * 2 / 3)
        QK_SCALE = 8.0

        def shift_tokens(t):
            a, s = jnp.split(t, 2, -1)
            s = jnp.pad(s, ((0, 0), (1, 0), (0, 0)))[:, :-1]
            return jnp.concatenate([a, s], -1)

        def l2norm(t):
            return t / jnp.maximum(jnp.linalg.norm(t, axis=-1, keepdims=True), 1e-12)

        def rotate_half(x):
            x1, x2 = jnp.split(x, 2, -1)
            return jnp.concatenate([-x2, x1], -1)

        def rotary_tables(n):
            half = jnp.arange(0, DIM_HEAD, 2, dtype=jnp.float32)
            inv_freq = 1.0 / 10000.0 ** (half / DIM_HEAD)
            t = jnp.arange(n, dtype=jnp.float32)
            freqs = t[:, None] * inv_freq[None, :]
            freqs = jnp.concatenate([freqs, freqs], -1)
            base_scale = (half + 0.4 * DIM_HEAD) / (1.4 * DIM_HEAD)
            power = (t - n // 2) / (WINDOW // 2)
            scale = base_scale[None, :] ** power[:, None]
            scale = jnp.concatenate([scale, scale], -1)
            return (freqs, scale)

        def local_attention(q, k, v):
            b, h, n, d = q.shape
            w = WINDOW
            nw = n // w
            bq = q.reshape(b, h, nw, w, d)
            bk = k.reshape(b, h, nw, w, d)
            bv = v.reshape(b, h, nw, w, d)

            def look(t):
                p = jnp.pad(t, ((0, 0), (0, 0), (1, 0), (0, 0), (0, 0)))
                return jnp.concatenate([p[:, :, :nw], p[:, :, 1:]], axis=3)
            bk2, bv2 = (look(bk), look(bv))
            seq = jnp.arange(n).reshape(nw, w)
            seq_p = jnp.pad(seq, ((1, 0), (0, 0)), constant_values=-1)
            jt = jnp.concatenate([seq_p[:nw], seq_p[1:]], axis=1)
            it = seq[:, :, None]
            jb = jt[:, None, :]
            mask = (it < jb) | (it > jb + w) | (jb == -1)
            sim = jnp.einsum('bhwie,bhwje->bhwij', bq, bk2) * QK_SCALE
            sim = jnp.where(mask, -jnp.finfo(sim.dtype).max, sim)
            attn = jax.nn.softmax(sim, -1)
            out = jnp.einsum('bhwij,bhwje->bhwie', attn, bv2)
            return out.reshape(b, h, n, d)

        def attn_layer(x, Wqkv, qs, ksc, Wo):
            b, n, _ = x.shape
            qkv = x @ Wqkv
            q, k, v = jnp.split(qkv, 3, -1)
            sh = lambda t: t.reshape(b, n, HEADS, DIM_HEAD).transpose(0, 2, 1, 3)
            q, k, v = (sh(q), sh(k), sh(v))
            q = l2norm(q) * qs
            k = l2norm(k) * ksc
            freqs, scale = rotary_tables(n)
            cos, sin = (jnp.cos(freqs), jnp.sin(freqs))
            q = q * cos * scale + rotate_half(q) * sin * scale
            inv = 1.0 / scale
            k = k * cos * inv + rotate_half(k) * sin * inv
            out = local_attention(q, k, v)
            out = out.transpose(0, 2, 1, 3).reshape(b, n, INNER)
            return out @ Wo

        def ffn_layer(x, g, bln, W1, b1, W2, b2):
            mu = x.mean(-1, keepdims=True)
            var = ((x - mu) ** 2).mean(-1, keepdims=True)
            xn = (x - mu) / jnp.sqrt(var + 1e-05) * g + bln
            hg = xn @ W1 + b1
            a, gate = jnp.split(hg, 2, -1)
            return a * jax.nn.gelu(gate, approximate=False) @ W2 + b2
        for i in range(DEPTH):
            x = attn_layer(shift_tokens(x), Wqkv[i], q_scale[i], k_scale[i], Wo[i]) + x
            x = ffn_layer(shift_tokens(x), ln_g[i], ln_b[i], W1[i], b1[i], W2[i], b2[i]) + x
        return x
    x = x + _L0_attn_ref(_layernorm(x, axis=-1), L0_attn_params, L0_attn_Wv, L0_attn_bv, L0_attn_Wo, L0_attn_bo)
    x = x + _L0_xattn_ref(_layernorm(x, axis=-1), ctx_1024, mask_BxS2_bk0, L0_xattn_W_Q, L0_xattn_W_K, L0_xattn_W_V, L0_xattn_W_O)
    x = x + _L0_ffn_ref(_layernorm(x, axis=-1), L0_ffn_Wqkv, L0_ffn_q_scale, L0_ffn_k_scale, L0_ffn_Wo, L0_ffn_ln_g, L0_ffn_ln_b, L0_ffn_W1, L0_ffn_b1, L0_ffn_W2, L0_ffn_b2)
    return x

_drawn_inputs = setup_inputs


def setup_inputs(seed=0):
    import zlib

    import numpy as np

    out = dict(_drawn_inputs(seed))
    spreads = {'L0_ffn_q_scale': (1.0, 0.6),
     'L0_ffn_k_scale': (1.0, 0.6),
     'L0_ffn_ln_g': (1.0, 0.6),
     'L0_ffn_ln_b': (0.0, 0.8),
     'L0_ffn_b1': (0.0, 0.8),
     'L0_ffn_b2': (0.0, 0.1)}
    factors = {'L0_attn_bv': 8.0, 'L0_ffn_W1': 3.725, 'L0_ffn_W2': 3.662}
    for name, (base, spread) in spreads.items():
        noise = np.random.default_rng([zlib.crc32(name.encode()), seed]).standard_normal(out[name].shape)
        drawn = base * np.exp(spread * noise) if base else spread * noise
        out[name] = jnp.asarray(drawn.astype(out[name].dtype))
    for name, factor in factors.items():
        out[name] = (out[name] * factor).astype(out[name].dtype)
    return out
```

```python
import numpy as np
from contextlib import ExitStack

import concourse.bass as bass
from concourse import mybir

FP32, BF16, I32, U8 = mybir.dt.float32, mybir.dt.bfloat16, mybir.dt.int32, mybir.dt.uint8
ALU = mybir.AluOpType
ACT = mybir.ActivationFunctionType
AX = mybir.AxisListType

BATCH, SEQ, DIM = 64, 64, 128
TILES = BATCH * SEQ // 128
HEADS, PAIRS = 16, 8
HD = 64
SD = DIM // HEADS
DEPTH, WINDOW = 6, 32
INNER = HEADS * HD
FF = int(DIM * 4 * 2 / 3)
FF_CHUNKS = [(c * 128, min(128, FF - c * 128)) for c in range(3)]
MASKED = -1.0e37
RSQRT_MAGIC = float(0x5F3759DF)
EPS = 1e-5


class Names:
    pass


def at_least(eng, sem, value):
    if not isinstance(value, int) or value > 0:
        eng.wait_ge(sem, value)


def hold(eng, held):
    eng.sem_inc(held, 1)


def run_pipeline(eng, turn, tiles):
    turn(-1, 1, True, False, False, False)
    turn(0, 0, True, True, False, False)
    turn(1, 1, True, True, True, False)
    turn(2, 0, True, True, True, True)
    turn(3, 1, True, True, True, True)
    with eng.Fori(4, tiles - 3, 2) as i:
        turn(i, 0, True, True, True, True)
        turn(i + 1, 1, True, True, True, True)
    turn(tiles - 2, 0, True, True, True, True)
    turn(tiles - 1, 1, False, True, True, True)
    turn(tiles, 0, False, False, True, True)
    turn(tiles + 1, 1, False, False, False, True)


def flat(ap):
    return ap.rearrange("p a b -> p (a b)")


def build(nc, x, ctx_in, mask, params, wvT, bv, woT_a, bo, wq, wk, wv, wo_x, wqkv, q_scale, k_scale, wo,
          ln_gT, ln_bT, w1, b1T, w2, b2, c_ident, c_shift, c_causal, c_rot, c_heads8, out):
    es = ExitStack()
    with es:
        def sb(name, shape, dt=FP32):
            return es.enter_context(nc.sbuf_tensor(name, shape, dt))

        def sem(name):
            return es.enter_context(nc.semaphore(name))

        m = Names()
        m.x, m.ctx_in, m.mask, m.params, m.wvT, m.bv = x, ctx_in, mask, params, wvT, bv
        m.woT_a, m.bo, m.wq, m.wk, m.wv, m.wo_x = woT_a, bo, wq, wk, wv, wo_x
        m.wqkv, m.q_scale, m.k_scale, m.wo, m.ln_gT, m.ln_bT = wqkv, q_scale, k_scale, wo, ln_gT, ln_bT
        m.w1, m.b1T, m.w2, m.b2, m.c_ident, m.c_shift = w1, b1T, w2, b2, c_ident, c_shift
        m.c_causal, m.c_rot, m.c_heads8, m.out = c_causal, c_rot, c_heads8, out

        m.X = sb("X", [128, TILES, DIM])
        m.Y = sb("Y", [128, TILES, DIM])
        m.WA = sb("WA", [128, 3 * INNER])
        m.WO = sb("WO", [128, PAIRS * DIM])
        m.W1 = sb("W1", [128, 2 * FF])
        m.W2 = sb("W2", [128, 3 * DIM])
        m.ident = sb("ident", [128, 128])
        m.identb = sb("identb", [128, 128], BF16)
        m.shift = sb("shift", [128, 128])
        m.causal = sb("causal", [128, 512])
        m.causalb = sb("causalb", [128, 512], BF16)
        m.rot = sb("rot", [128, 2, 2, HD])
        m.scales = sb("scales", [128, 2, 2, DEPTH, HD])
        m.tables = sb("tables", [128, DEPTH, 2, 2, HD])
        m.heads8 = sb("heads8", [128, HEADS])
        m.gcol = sb("gcol", [128, DEPTH])
        m.bcol = sb("bcol", [128, DEPTH])
        m.b1col = sb("b1col", [128, 2, 3, DEPTH])
        m.ones = sb("ones", [1, 128])
        m.onesb = sb("onesb", [1, 128], BF16)
        m.minus_half = sb("minus_half", [128, 1])
        m.bvrow = sb("bvrow", [1, DIM])
        m.borow = sb("borow", [1, DIM])
        m.tril = sb("tril", [128, SD])
        m.trilbd = sb("trilbd", [128, 128])
        m.trilT = sb("trilT", [128, 128])
        m.wqk = sb("wqk", [128, 128])
        m.wvT_sb = sb("wvT_sb", [128, 128])
        m.woT_sb = sb("woT_sb", [128, 128])
        m.mask8 = sb("mask8", [1, BATCH * SEQ // 4], I32)
        m.maskb = sb("maskb", [1, BATCH * SEQ], BF16)
        m.maskrow = sb("maskrow", [1, 2, 4, 128], BF16)
        m.ctx_sb = sb("ctx_sb", [128, 2, DIM])
        m.ystat = sb("ystat", [128, DIM])
        m.xsT = sb("xsT", [128, 2, SEQ])
        m.xsT_shifted = sb("xsT_shifted", [128, 2, SEQ])
        m.ctxT = sb("ctxT", [128, 128])
        m.sq = sb("sq", [128, 2048])
        m.ss = sb("ss", [128, 32])
        m.ssm = sb("ssm", [128, 32])
        m.bits = sb("bits", [128, 32], I32)
        m.seed = sb("seed", [128, 32], I32)
        m.rn = sb("rn", [128, 32])
        m.rn_a = sb("rn_a", [128, 32])
        m.rn_b = sb("rn_b", [128, 32])
        m.qn = sb("qn", [128, 2048])
        m.RA = sb("RA", [128, 2048])
        m.RB = sb("RB", [128, 2048])
        m.qTbd = sb("qTbd", [128, PAIRS, 2, 2, SEQ])
        m.kT = sb("kT", [128, PAIRS * 128])
        m.V = sb("V", [128, 2, HEADS * (HD + 1)])
        m.Vself = sb("Vself", [128, 2, HEADS * (SD + 1)])
        m.D = sb("D", [128, 1024])
        m.P = sb("P", [128, 1024])
        m.mx = sb("mx", [128, 16])
        m.PTbd = sb("PTbd", [128, HEADS, 2, SEQ])
        m.rs = sb("rs", [128, HEADS])
        m.On = sb("On", [128, HEADS * HD])
        m.OT = sb("OT", [128, PAIRS * 128])
        m.y1 = sb("y1", [128, 2, DIM])
        m.ys = sb("ys", [128, DIM])
        m.stats = sb("stats", [128, 6])
        m.mv = sb("mv", [128, 2])
        m.vare = sb("vare", [128, 1])
        m.rstd = sb("rstd", [128, 1])
        m.xn = sb("xn", [128, DIM])
        m.xnT = sb("xnT", [128, 2, 128])
        m.G = sb("G", [128, 3, 256])
        m.H = sb("H", [128, 3, 256])
        m.bank = [es.enter_context(nc.psum_tensor(f"bank{n}", [128, 512], FP32)) for n in range(8)]

        m.cross_w = sem("cross_weights")

        setup(nc, sem, m)
        for kind in ("self", "cross", "local"):
            stage(nc, sem, kind, m)
        finish(nc, sem, m)


def setup(nc, sem, m):
    dma, dmac = sem("setup_dma"), sem("setup_tril_zero")
    cast, zeroed, made = sem("setup_cast"), sem("setup_zeroed"), sem("setup_made")
    tril_done, tril_copied, norm = sem("setup_tril_done"), sem("setup_tril_copied"), sem("setup_norm")
    held = sem("setup_held")
    var, rstd_done, small = sem("setup_var"), sem("setup_rstd"), sem("setup_small")
    loads = [
        (m.X[:, :, :], m.x.rearrange("(t b) s d -> (b s) t d", b=2)),
        (m.ident[:, :], m.c_ident), (m.shift[:, :], m.c_shift), (m.causal[:, :], m.c_causal),
        (m.rot[:, :, :, :], m.c_rot), (m.heads8[:, :], m.c_heads8),
        (m.gcol[:, :], m.ln_gT), (m.bcol[:, :], m.ln_bT), (m.bvrow[:, :], m.bv), (m.borow[:, :], m.bo),
        (m.wvT_sb[:, :], m.wvT), (m.woT_sb[:, :], m.woT_a), (m.mask8[:, :], m.mask),
    ]
    for side in range(2):
        for c, (at, rows) in enumerate(FF_CHUNKS):
            loads.append((m.b1col[0:rows, side, c, :], m.b1T[side * FF + at:side * FF + at + rows, :]))
    half = HD // 2
    for n, s in enumerate((m.q_scale, m.k_scale)):
        wide = s.rearrange("l (a d) -> a l d", a=1)
        loads.append((m.scales[:, n, 0, :, :], wide.to_broadcast([128, DEPTH, HD])))
        for to, frm in ((0, half), (half, 0)):
            loads.append((m.scales[:, n, 1, :, to:to + half],
                          wide[:, :, frm:frm + half].to_broadcast([128, DEPTH, half])))
    with nc.Block() as block:

        @block.sync
        def _(sp):
            for dst, src in loads:
                sp.dma_start(dst, src).then_inc(dma, 16)
            sp.wait_ge(dmac, 1)
            for i in range(SD):
                off = i * (i + 1) // 2
                sp.dma_start(m.tril[i:128:SD, 0:i + 1], m.params[:, off:off + i + 1],
                             allow_slow_non_contiguous=True).then_inc(tril_done, 16)

        @block.gpsimd
        def _(pool):
            pool.memset(m.tril[:, :], 0.0).then_inc(dmac, 1)
            pool.memset(m.ones[:, :], 1.0)
            pool.memset(m.onesb[:, :], 1.0)
            pool.memset(m.minus_half[:, :], -0.5).then_inc(zeroed, 1)
            pool.memset(m.qTbd[:, :, :, :, :], 0.0)
            pool.memset(m.PTbd[:, :, :, :], 0.0)
            pool.memset(m.H[:, :, :], 1.0)
            pool.memset(m.V[:, :, :], 1.0)
            pool.memset(m.Vself[:, :, :], 1.0)
            pool.memset(m.xsT_shifted[:, :, :], 0.0)

            def inverse_root(t):
                at_least(pool, rstd_done, t)
                pool.wait_ge(var, t + 1)
                hold(pool, held)
                pool.tensor_scalar(m.vare[:, :], m.mv[:, 1:2], EPS, None, ALU.add).then_inc(small, 1)
                pool.wait_ge(small, t + 1)
                pool.tensor_tensor(m.rstd[:, :], m.vare[:, :], m.minus_half[:, :], ALU.pow).then_inc(rstd_done, 1)

            inverse_root(0)
            with pool.Fori(1, TILES, 1) as t:
                inverse_root(t)

        @block.vector
        def _(dve):
            dve.wait_ge(dma, 16 * len(loads))
            dve.tensor_copy(m.identb[:, :], m.ident[:, :]).then_inc(cast, 1)
            dve.tensor_copy(m.causalb[:, :], m.causal[:, :]).then_inc(cast, 1)
            dve.tensor_scalar(m.maskb[:, :], m.mask8[:, :].bitcast(U8), MASKED, None, ALU.mult).then_inc(cast, 1)
            for n in range(2):
                for s in range(2):
                    dve.tensor_tensor(m.tables[:, :, n, s, :], m.scales[:, n, s, :, :],
                                      m.rot[:, n, s, :].unsqueeze(1).to_broadcast([128, DEPTH, HD]), ALU.mult)
            dve.wait_ge(tril_done, 16 * SD)
            dve.tensor_tensor(m.trilbd[:, :].rearrange("p (h j) -> p h j", j=SD),
                              m.tril[:, :].unsqueeze(1).to_broadcast([128, HEADS, SD]),
                              m.heads8[:, :].unsqueeze(2).to_broadcast([128, HEADS, SD]), ALU.mult).then_inc(made, 1)

            def normalise(t):
                at_least(dve, norm, t)
                hold(dve, held)
                dve.bn_stats(m.stats[:, :], m.X[:, bass.ds(t, 1), :]).then_inc(cast, 1)
                dve.wait_ge(cast, t + 4)
                hold(dve, held)
                dve.bn_aggr(m.mv[:, :], m.stats[:, :]).then_inc(var, 1)
                dve.wait_ge(rstd_done, t + 1)
                dve.tensor_scalar(m.Y[:, bass.ds(t, 1), :], m.X[:, bass.ds(t, 1), :], m.mv[:, 0:1], m.rstd[:, 0:1],
                                  ALU.subtract, ALU.mult).then_inc(norm, 1)

            normalise(0)
            with dve.Fori(1, TILES, 1) as t:
                normalise(t)

        @block.tensor
        def _(pe):
            pe.wait_ge(made, 1)
            pe.transpose(m.bank[0][:, 0:128], m.trilbd[:, :], m.ident[:, :]).then_inc(tril_copied, 1)
            pe.wait_ge(made, 2)
            pe.matmul(m.bank[1][:, 0:128], m.trilT[:, :], m.trilT[:, :], start=True, stop=True).then_inc(tril_copied, 1)

        @block.scalar
        def _(act):
            act.wait_ge(tril_copied, 1)
            act.activation(m.trilT[:, :], m.bank[0][:, 0:128], ACT.Copy).then_inc(made, 1)
            act.wait_ge(tril_copied, 2)
            act.activation(m.wqk[:, :], m.bank[1][:, 0:128], ACT.Copy).then_inc(made, 1)


def finish(nc, sem, m):
    summed, stored = sem("finish_summed"), sem("finish_stored")
    parts = 4
    n = TILES // parts
    out = m.out.rearrange("(t b) s d -> (b s) t d", b=2)
    with nc.Block() as block:

        @block.vector
        def _(dve):
            for c in range(parts):
                part = slice(c * n, (c + 1) * n)
                dve.tensor_tensor(m.X[:, part, :], m.X[:, part, :], m.Y[:, part, :], ALU.add).then_inc(summed, 1)

        @block.sync
        def _(sp):
            for c in range(parts):
                part = slice(c * n, (c + 1) * n)
                sp.wait_ge(summed, c + 1)
                sp.dma_start(out[:, part, :], m.X[:, part, :]).then_inc(stored, 16)
            sp.wait_ge(stored, 16 * parts)


def stage(nc, sem, kind, m):
    SELF, CROSS, LOCAL = kind == "self", kind == "cross", kind == "local"
    N = TILES * DEPTH if LOCAL else TILES
    DV = SD if SELF else HD
    EXP_SCALE = {"self": SD ** -0.5, "cross": HD ** -0.5, "local": 8.0}[kind]
    OGROUPS = [(6, 0, 16)] if SELF else [(6, 0, 7), (7, 7, 14), (4, 14, 16)]
    NO = len(OGROUPS)
    NPRE = 1 if SELF else 2
    NQK = 1 if SELF else 4
    NQT, NKT = (2, 1) if SELF else (4, 2)
    NV = NOT = 1 if SELF else 2
    NRN = 12
    b = m.bank
    s = Names()
    s.w_in = sem(f"{kind}_w_in")
    s.w_out = sem(f"{kind}_w_out")
    s.ystat = sem(f"{kind}_ystat")
    s.pre_t = sem(f"{kind}_pre_t")
    s.pre_copied = sem(f"{kind}_pre_copied")
    s.qk = sem(f"{kind}_qk")
    s.qT = sem(f"{kind}_qT")
    s.kT = sem(f"{kind}_kT")
    s.v = sem(f"{kind}_v")
    s.v_copied = sem(f"{kind}_v_copied")
    s.scores = sem(f"{kind}_scores")
    s.mx = sem(f"{kind}_mx")
    s.diff = sem(f"{kind}_diff")
    s.probs = sem(f"{kind}_probs")
    s.pt = sem(f"{kind}_pt")
    s.pt_copied = sem(f"{kind}_pt_copied")
    s.o = sem(f"{kind}_o")
    s.recip = sem(f"{kind}_recip")
    s.onorm = sem(f"{kind}_onorm")
    s.ot = sem(f"{kind}_ot")
    s.ot_copied = sem(f"{kind}_ot_copied")
    s.wo = sem(f"{kind}_wo")
    s.y1 = sem(f"{kind}_y1")
    s.stats = sem(f"{kind}_stats")
    s.var = sem(f"{kind}_var")
    s.vare = sem(f"{kind}_vare")
    s.rstd = sem(f"{kind}_rstd")
    s.xn = sem(f"{kind}_xn")
    if CROSS:
        s.ctx_even = sem(f"{kind}_ctx_even")
        s.ctx_odd = sem(f"{kind}_ctx_odd")
        s.mask_made = sem(f"{kind}_mask_made")
    if LOCAL:
        s.w_ff = sem(f"{kind}_w_ff")
        s.sq = sem(f"{kind}_sq")
        s.ss = sem(f"{kind}_ss")
        s.seed = sem(f"{kind}_seed")
        s.newton = sem(f"{kind}_newton")
        s.qn = sem(f"{kind}_qn")
        s.ra = sem(f"{kind}_ra")
        s.rb = sem(f"{kind}_rb")
        s.rot = sem(f"{kind}_rot")
        s.sh = sem(f"{kind}_sh")
        s.sh_copied = sem(f"{kind}_sh_copied")
        s.ys = sem(f"{kind}_ys")
        s.xn_t = sem(f"{kind}_xn_t")
        s.xn_copied = sem(f"{kind}_xn_copied")
        s.ff = sem(f"{kind}_ff")
        s.gelu = sem(f"{kind}_gelu")
        s.h = sem(f"{kind}_h")
        s.w2 = sem(f"{kind}_w2")
        s.y = sem(f"{kind}_y")
    held = sem(f"{kind}_held")
    V = m.Vself if SELF else m.V
    qTbd = m.RA[:, :].rearrange("p (h t a q) -> p h t a q", h=PAIRS, t=2, a=2) if SELF else m.qTbd
    xsT_tokens = m.xsT_shifted if LOCAL else m.xsT
    xsT = flat(xsT_tokens[:, :, :])

    def slot(t):
        return t % TILES if LOCAL else t

    def tile_of(buf, t):
        return flat(buf[:, bass.ds(slot(t), 1), :])

    with nc.Block() as block:

        @block.sync
        def _(sp):
            if SELF:
                for c, w in enumerate((m.wq, m.wk, m.wv)):
                    sp.dma_start(m.WA[:, c * INNER:(c + 1) * INNER], w).then_inc(m.cross_w, 16)
                sp.dma_start(m.WO[:, :].rearrange("p (c n) -> p c n", n=DIM),
                             m.wo_x.rearrange("(c p) n -> p c n", p=128)).then_inc(m.cross_w, 16)
            if CROSS:
                ctx_tiles = m.ctx_in.rearrange("(t b) s d -> t (b s) d", b=2)

                def load_ctx(t, par):
                    at_least(sp, s.pre_t, t - 1)
                    sp.dma_start(m.ctx_sb[:, par, :], flat(ctx_tiles[bass.ds(t, 1), :, :].rearrange("a p d -> p a d")))\
                      .then_inc((s.ctx_even, s.ctx_odd)[par], 16)

                load_ctx(0, 0)
                load_ctx(1, 1)
                with sp.Fori(2, N - 1, 2) as t:
                    load_ctx(t, 0)
                    load_ctx(t + 1, 1)
            if LOCAL:
                def load_in(l):
                    sp.dma_start(m.WA[:, :], flat(m.wqkv[bass.ds(l, 1), :, :].rearrange("a p n -> p a n")))\
                      .then_inc(s.w_in, 16)

                def load_out(l):
                    sp.dma_start(m.WO[:, :].rearrange("p (c n) -> p c n", n=DIM),
                                 m.wo[bass.ds(l, 1), :, :].rearrange("a (c p) n -> p (a c) n", p=128)).then_inc(s.w_out, 16)

                def load_ff(l):
                    at, rows = FF_CHUNKS[2]
                    one = bass.ds(l, 1)
                    sp.dma_start(m.W1[:, :], flat(m.w1[one, :, :].rearrange("a p n -> p a n"))).then_inc(s.w_ff, 16)
                    sp.dma_start(m.W2[:, 0:2 * DIM].rearrange("p (c n) -> p c n", n=DIM),
                                 m.w2[one, 0:at, :].rearrange("a (c p) n -> p (a c) n", p=128)).then_inc(s.w_ff, 16)
                    sp.dma_start(m.W2[0:rows, 2 * DIM:3 * DIM],
                                 flat(m.w2[one, at:FF, :].rearrange("a p n -> p a n"))).then_inc(s.w_ff, 16)
                    sp.dma_start(m.W2[rows:rows + 1, 2 * DIM:3 * DIM], m.b2[one, :]).then_inc(s.w_ff, 16)

                load_in(0)
                load_out(0)
                load_ff(0)
                with sp.Fori(1, DEPTH, 1) as l:
                    sp.wait_ge(s.v, NV * TILES * l)
                    load_in(l)
                    sp.wait_ge(s.wo, TILES * l)
                    load_out(l)
                    sp.wait_ge(s.w2, TILES // 2 * l)
                    load_ff(l)

        @block.tensor
        def _(pe):
            mm = nc.tensor.matmul

            def out_projection(t):
                pe.wait_ge(s.ot_copied, NOT * (t + 1))
                if SELF:
                    mm(b[7][:, 0:128], m.OT[:, 0:128], m.woT_sb[:, :], start=True, stop=False)
                    mm(b[7][:, 0:128], m.ones[:, :], m.borow[:, :], start=False, stop=True).then_inc(s.wo, 1)
                    return
                if LOCAL:
                    pe.wait_ge(s.w_out, 16 * (t // TILES) + 16)
                for c in range(PAIRS):
                    last = mm(b[7][:, 0:128], m.OT[:, c * 128:(c + 1) * 128], m.WO[:, c * 128:(c + 1) * 128],
                              start=(c == 0), stop=(c == PAIRS - 1))
                last.then_inc(s.wo, 1)

            def queries_keys(t):
                pe.wait_ge(s.pre_copied, NPRE * (t + 1))
                at_least(pe, s.qT, NQT * t)
                at_least(pe, s.kT, NKT * t)
                if SELF:
                    mm(b[0][:, 0:128], m.wqk[:, :], xsT, start=True, stop=True).then_inc(s.qk, 1)
                if CROSS:
                    if isinstance(t, int) and t == 0:
                        pe.wait_ge(m.cross_w, 64)
                    for c in range(4):
                        for n in range(4):
                            at = c * 512 + n * 128
                            last = mm(b[c][:, n * 128:(n + 1) * 128], m.WA[:, at:at + 128],
                                      xsT if c < 2 else m.ctxT[:, :], start=True, stop=True)
                        last.then_inc(s.qk, 1)
                if LOCAL:
                    pe.wait_ge(s.w_in, 16 * (t // TILES) + 16)
                    for c in range(4):
                        mm(b[c][:, :], xsT, m.WA[:, c * 512:(c + 1) * 512], start=True, stop=True).then_inc(s.qk, 1)

            def values(t):
                if SELF:
                    mm(b[6][:, 0:128], xsT, m.wvT_sb[:, :], start=True, stop=False)
                    mm(b[6][:, 0:128], m.ones[:, :], m.bvrow[:, :], start=False, stop=True).then_inc(s.v, 1)
                    return
                for c in range(2):
                    at = 2 * INNER + c * 512
                    mm(b[6 + c][:, :], xsT if LOCAL else m.ctxT[:, :], m.WA[:, at:at + 512],
                       start=True, stop=True).then_inc(s.v, 1)

            def scores(t, par):
                pe.wait_ge(s.qT, NQT * (t + 1))
                pe.wait_ge(s.kT, NKT * (t + 1))
                if CROSS:
                    pe.wait_ge(s.mask_made, t + 1)
                for j in range(2):
                    if CROSS:
                        mm(b[4 + j][:, :], m.onesb[:, :], m.maskrow[:, par, :, :].rearrange("p a k -> p (a k)"),
                           start=True, stop=False)
                    if LOCAL:
                        mm(b[4 + j][:, :], m.identb[:, :], m.causalb[:, :], start=True, stop=False)
                    for n in range(8):
                        hp, bb = 4 * j + n // 2, n % 2
                        keys = bb * 64 if SELF else hp * 128 + bb * 64
                        last = mm(b[4 + j][:, n * 64:(n + 1) * 64], flat(qTbd[:, hp, bb, :, :]),
                                  m.kT[:, keys:keys + 64], start=SELF, stop=SELF or n == 7)
                    last.then_inc(s.scores, 1)

            def probs_transposed(t):
                for j in range(2):
                    pe.wait_ge(s.probs, 2 * t + j + 1)
                    for n in range(4):
                        c = 4 * j + n
                        last = nc.tensor.transpose(b[4 + j][:, n * 128:(n + 1) * 128], m.P[:, c * 128:(c + 1) * 128],
                                                   m.ident[:, :])
                    last.then_inc(s.pt, 1)

            def rotated_transposed(t):
                for j in range(4):
                    pe.wait_ge(s.ra, 4 * t + j + 1)
                    pe.wait_ge(s.rb, 4 * t + j + 1)
                    for n in range(4):
                        at, col = j * 512 + n * 128, n * 128
                        mm(b[j][:, col:col + 128], m.RA[:, at:at + 128], m.ident[:, :], is_transpose=True,
                           start=True, stop=False)
                        last = mm(b[j][:, col:col + 128], m.RB[:, at:at + 128], m.ident[:, :], is_transpose=True,
                                  start=False, stop=True)
                    last.then_inc(s.rot, 1)

            def head_outputs(t, par):
                pe.wait_ge(s.v_copied, NV * (t + 1))
                for bk, h0, h1 in OGROUPS:
                    pe.wait_ge(s.pt_copied, 4 * t + (2 if h1 <= PAIRS else 4))
                    for h in range(h0, h1):
                        at = (h - h0) * (DV + 1)
                        last = mm(b[bk][:, at:at + DV + 1], flat(m.PTbd[:, h, :, :]),
                                  V[:, par, h * (DV + 1):(h + 1) * (DV + 1)], start=True, stop=True)
                    last.then_inc(s.o, 1)

            def outputs_transposed(t):
                pe.wait_ge(s.onorm, NO * (t + 1))
                for j in range(NOT):
                    for n in range(1 if SELF else 4):
                        c = 4 * j + n
                        last = nc.tensor.transpose(b[4 + j][:, n * 128:(n + 1) * 128], m.On[:, c * 128:(c + 1) * 128],
                                                   m.ident[:, :])
                    last.then_inc(s.ot, 1)

            def pre_transposed(t, par):
                pe.wait_ge(s.ystat, t + 1)
                last = nc.tensor.transpose(b[5][:, 0:128], m.ystat[:, :], m.ident[:, :])
                if CROSS:
                    pe.wait_ge((s.ctx_even, s.ctx_odd)[par], 16 * ((t - par) // 2) + 16)
                    last = nc.tensor.transpose(b[5][:, 128:256], m.ctx_sb[:, par, :], m.ident[:, :])
                last.then_inc(s.pre_t, 1)

            def feed_forward_in(t):
                pe.wait_ge(s.xn_copied, t + 1)
                pe.wait_ge(s.w_ff, 64 * (t // TILES) + 64)
                for c, (at, rows) in enumerate(FF_CHUNKS):
                    bk = b[7 - c % 2]
                    if c == 2:
                        pe.wait_ge(s.h, 3 * ((t - 1) // 2) + 1)
                    for side, off in ((0, FF), (1, 0)):
                        last = mm(bk[0:rows, side * 256:(side + 1) * 256], m.W1[:, off + at:off + at + rows],
                                  flat(m.xnT[:, :, :]), start=True, stop=True)
                    last.then_inc(s.ff, 1)

            def feed_forward_out(t):
                pe.wait_ge(s.h, 3 * ((t - 1) // 2) + 3)
                for n in range(2):
                    for c, (_, rows) in enumerate(FF_CHUNKS):
                        k = rows + (c == 2)
                        last = mm(b[7][:, n * 128:(n + 1) * 128], m.H[0:k, c, n * 128:(n + 1) * 128],
                                  m.W2[0:k, c * 128:(c + 1) * 128], start=(c == 0), stop=(c == 2))
                last.then_inc(s.w2, 1)

            def turn(i, par, pre, head, mid, tail):
                if tail:
                    out_projection(i - 2)
                if head:
                    queries_keys(i)
                if tail and LOCAL:
                    pe.wait_ge(s.y1, i - 1)
                    mm(b[7][:, 0:64], m.shift[:, :], m.y1[:, par, 64:128], start=True, stop=True).then_inc(s.sh, 1)
                if mid:
                    scores(i - 1, 1 - par)
                if head:
                    if tail:
                        pe.wait_ge(s.sh_copied if LOCAL else s.y1, i - 1)
                    values(i)
                if tail and LOCAL:
                    pe.wait_ge(s.xn, i - 1)
                    if head:
                        pe.wait_ge(s.v_copied, NV * (i + 1))
                    nc.tensor.transpose(b[6][:, 0:128], m.xn[:, :], m.ident[:, :]).then_inc(s.xn_t, 1)
                if mid:
                    probs_transposed(i - 1)
                if tail and LOCAL and par == 1:
                    feed_forward_in(i - 2)
                if head and LOCAL:
                    rotated_transposed(i)
                if tail and LOCAL and par == 1:
                    feed_forward_out(i - 2)
                if mid:
                    if head:
                        pe.wait_ge(s.v_copied, NV * (i + 1))
                    if tail:
                        if not LOCAL:
                            pe.wait_ge(s.y1, i - 1)
                        elif par == 1:
                            pe.wait_ge(s.y, TILES // 2 + (i - 3) // 2 + 1)
                        else:
                            pe.wait_ge(s.xn_copied, i - 1)
                    head_outputs(i - 1, 1 - par)
                if pre:
                    pre_transposed(i + 1, 1 - par)
                if mid:
                    if pre:
                        pe.wait_ge(s.pre_copied, NPRE * (i + 2))
                    outputs_transposed(i - 1)

            run_pipeline(pe, turn, N)

        @block.scalar
        def _(act):
            def copy(dst, src):
                return nc.scalar.activation(dst, src, ACT.Copy)

            def turn(i, par, pre, head, mid, tail):
                if head and LOCAL:
                    for j in range(4):
                        act.wait_ge(s.qk, 4 * i + j + 1)
                        at_least(act, s.ss, 4 * (i - 1) + j + 1)
                        nc.scalar.activation(m.sq[:, j * 512:(j + 1) * 512], b[j][:, :], ACT.Square).then_inc(s.sq, 1)
                if tail and LOCAL:
                    act.wait_ge(s.sh, i - 1)
                    at_least(act, s.xn, i - 2)
                    copy(m.ys[:, 64:128], b[7][:, 0:64]).then_inc(s.sh_copied, 1)
                if head:
                    for j in range(NV):
                        act.wait_ge(s.v, NV * i + j + 1)
                        n = HEADS if SELF else PAIRS
                        dst = V[:, par, :].rearrange("p (h d) -> p h d", d=DV + 1)
                        copy(dst[:, j * n:(j + 1) * n, 0:DV],
                             b[6 + j][:, 0:n * DV].rearrange("p (h d) -> p h d", d=DV)).then_inc(s.v_copied, 1)
                    if SELF:
                        at_least(act, s.scores, 2 * i)
                        act.wait_ge(s.pre_copied, i + 1)
                        copy(m.kT[:, 0:128], xsT).then_inc(s.kT, 1)
                if mid:
                    for j in range(2):
                        act.wait_ge(s.diff, 2 * (i - 1) + j + 1)
                        nc.scalar.activation(m.P[:, j * 512:(j + 1) * 512], m.D[:, j * 512:(j + 1) * 512], ACT.Exp,
                                             scale=EXP_SCALE).then_inc(s.probs, 1)
                if head and CROSS:
                    queries_keys_out(i, s.qk)
                if tail and LOCAL:
                    act.wait_ge(s.xn_t, i - 1)
                    l = (i - 2) // TILES
                    nc.scalar.activation(m.xnT[:, par, :], b[6][:, 0:128], ACT.Identity, scale=m.gcol[:, bass.ds(l, 1)],
                                         bias=m.bcol[:, bass.ds(l, 1)]).then_inc(s.xn_copied, 1)
                if mid:
                    for j in range(2):
                        act.wait_ge(s.pt, 2 * (i - 1) + j + 1)
                        for bb in range(2):
                            rows = slice(64 * bb, 64 * bb + 64)
                            copy(m.PTbd[rows, 8 * j:8 * j + 8, bb, :],
                                 b[4 + j][rows, :].rearrange("p (h q) -> p h q", q=SEQ)).then_inc(s.pt_copied, 1)
                if tail and LOCAL and par == 1:
                    l = (i - 2) // TILES
                    at_least(act, s.h, 3 * ((i - 3) // 2))
                    for c, (_, rows) in enumerate(FF_CHUNKS):
                        act.wait_ge(s.ff, 3 * ((i - 3) // 2) + c + 1)
                        nc.scalar.activation(m.G[0:rows, c, :], b[7 - c % 2][0:rows, 0:256], ACT.Gelu,
                                             bias=m.b1col[0:rows, 1, c, bass.ds(l, 1)]).then_inc(s.gelu, 1)
                if head and LOCAL:
                    queries_keys_out(i, s.rot)
                if pre:
                    act.wait_ge(s.pre_t, i + 2)
                    if SELF:
                        at_least(act, s.kT, i + 1)
                    if LOCAL:
                        copy(xsT_tokens[0:64, :, :], b[5][0:64, 0:128].rearrange("p (a q) -> p a q", q=SEQ))\
                            .then_inc(s.pre_copied, 1)
                        copy(xsT_tokens[64:128, :, 1:SEQ], b[5][64:128, 0:128].rearrange("p (a q) -> p a q", q=SEQ)[:, :, 0:SEQ - 1])\
                            .then_inc(s.pre_copied, 1)
                    else:
                        copy(xsT, b[5][:, 0:128]).then_inc(s.pre_copied, 1)
                    if CROSS:
                        copy(m.ctxT[:, :], b[5][:, 128:256]).then_inc(s.pre_copied, 1)
                if mid:
                    for j in range(NOT):
                        act.wait_ge(s.ot, NOT * (i - 1) + j + 1)
                        n = 128 if SELF else 512
                        copy(m.OT[:, j * n:(j + 1) * n], b[4 + j][:, 0:n]).then_inc(s.ot_copied, 1)

            def queries_keys_out(i, ready):
                at_least(act, s.scores, 2 * i)
                for j in range(2):
                    act.wait_ge(ready, 4 * i + j + 1)
                    for a in range(2):
                        rows = slice(64 * a, 64 * a + 64)
                        copy(qTbd[rows, 4 * j:4 * j + 4, :, a, :],
                             b[j][rows, :].rearrange("p (h t q) -> p h t q", h=4, q=SEQ)).then_inc(s.qT, 1)
                for j in range(2):
                    act.wait_ge(ready, 4 * i + 2 + j + 1)
                    copy(m.kT[:, j * 512:(j + 1) * 512], b[2 + j][:, :]).then_inc(s.kT, 1)

            run_pipeline(act, turn, N)

        @block.vector
        def _(dve):
            tt = nc.vector.tensor_tensor

            def turn(i, par, pre, head, mid, tail):
                if tail:
                    if LOCAL:
                        dve.wait_ge(s.y, TILES // 2 + (i - 2) // 2)
                    dve.wait_ge(s.wo, i - 1)
                    src = tile_of(m.Y if LOCAL else m.X, i - 2)
                    dst = m.y1[:, par, :] if LOCAL else src
                    tt(dst, src, b[7][:, 0:128], ALU.add).then_inc(s.y1, 1)
                if head and SELF:
                    dve.wait_ge(s.qk, i + 1)
                    at_least(dve, s.scores, 2 * i)
                    for bb in range(2):
                        tt(qTbd[:, :, bb, :, :],
                           b[0][:, bb * 64:(bb + 1) * 64].unsqueeze(1).unsqueeze(1).to_broadcast([128, PAIRS, 2, SEQ]),
                           m.heads8[:, :].rearrange("p (a c) -> p a c", c=2).unsqueeze(3).to_broadcast([128, PAIRS, 2, SEQ]),
                           ALU.mult).then_inc(s.qT, 1)
                if head and LOCAL:
                    at_least(dve, s.seed, 3 * i)
                    for j in range(4):
                        dve.wait_ge(s.sq, 4 * i + j + 1)
                        nc.vector.tensor_reduce(m.ss[:, 8 * j:8 * j + 8],
                                                m.sq[:, j * 512:(j + 1) * 512].rearrange("p (h d) -> p h d", d=HD),
                                                AX.X, ALU.add).then_inc(s.ss, 1)
                    dve.wait_ge(s.ss, 4 * (i + 1))
                    at_least(dve, s.newton, NRN * i)
                    nc.vector.tensor_scalar(m.ssm[:, :], m.ss[:, :], 1e-24, None, ALU.max).then_inc(s.seed, 1)
                    dve.wait_ge(s.seed, 3 * i + 1)
                    nc.vector.tensor_scalar(m.bits[:, :], m.ssm[:, :].bitcast(I32), 1, None, ALU.arith_shift_right)\
                        .then_inc(s.seed, 1)
                    dve.wait_ge(s.seed, 3 * i + 2)
                    nc.vector.tensor_scalar(m.seed[:, :], m.bits[:, :], -1.0, RSQRT_MAGIC, ALU.mult, ALU.add)\
                        .then_inc(s.seed, 1)
                if mid:
                    for j in range(2):
                        at_least(dve, s.diff, 2 * (i - 2) + j + 1)
                        dve.wait_ge(s.scores, 2 * (i - 1) + j + 1)
                        rows = b[4 + j][:, :].rearrange("p (n k) -> p n k", k=SEQ)
                        nc.vector.tensor_reduce(m.mx[:, 8 * j:8 * j + 8], rows, AX.X, ALU.max).then_inc(s.mx, 1)
                        dve.wait_ge(s.mx, 2 * (i - 1) + j + 1)
                        tt(m.D[:, j * 512:(j + 1) * 512].rearrange("p (n k) -> p n k", k=SEQ), rows,
                           m.mx[:, 8 * j:8 * j + 8].unsqueeze(2).to_broadcast([128, 8, SEQ]), ALU.subtract)\
                            .then_inc(s.diff, 1)
                if tail:
                    at_least(dve, s.xn, i - 2)
                    if LOCAL:
                        dve.wait_ge(s.sh_copied, i - 1)
                        dve.wait_ge(s.ys, i - 1)
                    else:
                        dve.wait_ge(s.y1, i - 1)
                    hold(dve, held)
                    row = m.ys[:, :] if LOCAL else tile_of(m.X, i - 2)
                    nc.vector.bn_stats(m.stats[:, :], row).then_inc(s.stats, 1)
                    dve.wait_ge(s.stats, i - 1)
                    hold(dve, held)
                    nc.vector.bn_aggr(m.mv[:, :], m.stats[:, :]).then_inc(s.var, 1)
                    dve.wait_ge(s.rstd, i - 1)
                    nc.vector.tensor_scalar(m.xn[:, :] if LOCAL else tile_of(m.Y, i - 2), row, m.mv[:, 0:1], m.rstd[:, 0:1],
                                            ALU.subtract, ALU.mult).then_inc(s.xn, 1)
                if head and LOCAL:
                    dve.wait_ge(s.newton, NRN * (i + 1))
                    for j in range(4):
                        at_least(dve, s.ra, 4 * (i - 1) + j + 1)
                        at_least(dve, s.rb, 4 * (i - 1) + j + 1)
                        tt(m.qn[:, j * 512:(j + 1) * 512].rearrange("p (h d) -> p h d", d=HD),
                           b[j][:, :].rearrange("p (h d) -> p h d", d=HD),
                           m.rn[:, 8 * j:8 * j + 8].unsqueeze(2).to_broadcast([128, 8, HD]), ALU.mult).then_inc(s.qn, 1)
                    half = HD // 2
                    l = i // TILES
                    for j in range(4):
                        dve.wait_ge(s.qn, 4 * i + j + 1)
                        at_least(dve, s.rot, 4 * (i - 1) + j + 1)
                        src = m.qn[:, j * 512:(j + 1) * 512].rearrange("p (h d) -> p h d", d=HD)
                        dst = m.RB[:, j * 512:(j + 1) * 512].rearrange("p (h d) -> p h d", d=HD)
                        for to, frm in ((0, half), (half, 0)):
                            tab = m.tables[:, bass.ds(l, 1), j // 2, 1, to:to + half].to_broadcast([128, 8, half])
                            last = tt(dst[:, :, to:to + half], src[:, :, frm:frm + half], tab, ALU.mult)
                        last.then_inc(s.rb, 1)
                if tail and LOCAL and par == 1:
                    l = (i - 2) // TILES
                    for c, (_, rows) in enumerate(FF_CHUNKS):
                        dve.wait_ge(s.gelu, 3 * ((i - 3) // 2) + c + 1)
                        nc.vector.scalar_tensor_tensor(
                            out=m.H[0:rows, c, :], in0=b[7 - c % 2][0:rows, 256:512], scalar=m.b1col[0:rows, 0, c, bass.ds(l, 1)],
                            in1=m.G[0:rows, c, :], op0=ALU.add, op1=ALU.mult).then_inc(s.h, 1)
                    dve.wait_ge(s.w2, (i - 3) // 2 + 1)
                    pairs = m.Y[:, :, :].rearrange("p (t a) d -> p t (a d)", a=2)
                    tt(flat(pairs[:, bass.ds((i - 3) // 2 % (TILES // 2), 1), :]), flat(m.y1[:, :, :]), b[7][:, 0:256],
                       ALU.add).then_inc(s.y, 1)
                if mid:
                    for g, (bk, h0, h1) in enumerate(OGROUPS):
                        n = h1 - h0
                        src = b[bk][:, 0:n * (DV + 1)].rearrange("p (h d) -> p h d", d=DV + 1)
                        at_least(dve, s.onorm, NO * (i - 2) + g + 1)
                        dve.wait_ge(s.o, NO * (i - 1) + g + 1)
                        nc.vector.reciprocal(m.rs[:, h0:h1].unsqueeze(2), src[:, :, DV:DV + 1]).then_inc(s.recip, 1)
                        dve.wait_ge(s.recip, NO * (i - 1) + g + 1)
                        tt(m.On[:, h0 * DV:h1 * DV].rearrange("p (h d) -> p h d", d=DV), src[:, :, 0:DV],
                           m.rs[:, h0:h1].unsqueeze(2).to_broadcast([128, n, DV]), ALU.mult).then_inc(s.onorm, 1)

            if LOCAL:
                dve.sem_inc(s.y, TILES // 2)
            run_pipeline(dve, turn, N)

        @block.gpsimd
        def _(pool):
            tt = nc.gpsimd.tensor_tensor

            def turn(i, par, pre, head, mid, tail):
                if head and CROSS:
                    at_least(pool, s.scores, 2 * (i - 1))
                    hold(pool, held)
                    row = m.maskb[:, bass.ds(i * 128, 128)]
                    nc.gpsimd.tensor_copy(m.maskrow[:, par, :, :], row.unsqueeze(1).to_broadcast([1, 4, 128]))\
                        .then_inc(s.mask_made, 1)
                if tail:
                    if LOCAL:
                        pool.wait_ge(s.y1, i - 1)
                        at_least(pool, s.xn, i - 2)
                        hold(pool, held)
                        nc.gpsimd.tensor_copy(m.ys[:, 0:64], m.y1[:, par, 0:64]).then_inc(s.ys, 1)
                    at_least(pool, s.rstd, i - 2)
                    pool.wait_ge(s.var, i - 1)
                    hold(pool, held)
                    nc.gpsimd.tensor_scalar(m.vare[:, :], m.mv[:, 1:2], EPS, None, ALU.add).then_inc(s.vare, 1)
                    pool.wait_ge(s.vare, i - 1)
                    tt(m.rstd[:, :], m.vare[:, :], m.minus_half[:, :], ALU.pow).then_inc(s.rstd, 1)
                if head and LOCAL:
                    pool.wait_ge(s.seed, 3 * (i + 1))
                    at_least(pool, s.newton, NRN * i)
                    at_least(pool, s.qn, 4 * i)
                    y = m.seed[:, :].bitcast(FP32)
                    for step in range(3):
                        done = NRN * i + 4 * step
                        if step:
                            pool.wait_ge(s.newton, done)
                        tt(m.rn_a[:, :], y, y, ALU.mult).then_inc(s.newton, 1)
                        pool.wait_ge(s.newton, done + 1)
                        tt(m.rn_b[:, :], m.rn_a[:, :], m.ssm[:, :], ALU.mult).then_inc(s.newton, 1)
                        pool.wait_ge(s.newton, done + 2)
                        hold(pool, held)
                        nc.gpsimd.tensor_scalar(m.rn_a[:, :], m.rn_b[:, :], -0.5, 1.5, ALU.mult, ALU.add)\
                            .then_inc(s.newton, 1)
                        pool.wait_ge(s.newton, done + 3)
                        tt(m.rn[:, :], y, m.rn_a[:, :], ALU.mult).then_inc(s.newton, 1)
                        y = m.rn[:, :]
                    l = i // TILES
                    for j in range(4):
                        pool.wait_ge(s.qn, 4 * i + j + 1)
                        at_least(pool, s.rot, 4 * (i - 1) + j + 1)
                        hold(pool, held)
                        tab = m.tables[:, bass.ds(l, 1), j // 2, 0, :].to_broadcast([128, 8, HD])
                        tt(m.RA[:, j * 512:(j + 1) * 512].rearrange("p (h d) -> p h d", d=HD),
                           m.qn[:, j * 512:(j + 1) * 512].rearrange("p (h d) -> p h d", d=HD), tab, ALU.mult)\
                            .then_inc(s.ra, 1)
                if pre:
                    if LOCAL:
                        pool.wait_ge(s.y, (i + 1) // 2 + 1)
                    at_least(pool, s.pre_t, i + 1)
                    hold(pool, held)
                    nc.gpsimd.tensor_copy(m.ystat[:, :], tile_of(m.Y, i + 1)).then_inc(s.ystat, 1)

            run_pipeline(pool, turn, N)


def constants():
    f32 = np.float32
    c = {}
    c["c_ident"] = np.eye(128, dtype=f32)
    t = np.arange(128)
    c["c_shift"] = ((t[None, :] == t[:, None] + 1) & (t[None, :] % SEQ != 0)).astype(f32)
    q, k = t[:, None] % SEQ, np.arange(512)[None, :] % SEQ
    c["c_causal"] = np.where((k > q) | (q > k + WINDOW), f32(MASKED), f32(0))
    half = np.arange(0, HD, 2, dtype=f32)
    inv_freq = (1.0 / np.power(f32(10000.0), half / f32(HD))).astype(f32)
    pos = np.arange(SEQ, dtype=f32)
    freqs = np.tile(pos[:, None] * inv_freq[None, :], (1, 2)).astype(f32)
    base = ((half + f32(0.4 * HD)) / f32(1.4 * HD)).astype(f32)
    power = ((pos - SEQ // 2) / (WINDOW // 2)).astype(f32)
    scale = np.tile(np.power(base[None, :], power[:, None]), (1, 2)).astype(f32)
    cos, sin = np.cos(freqs), np.sin(freqs)
    sin[:, :HD // 2] *= -1
    rot = np.stack([np.stack([cos * scale, sin * scale], 1), np.stack([cos / scale, sin / scale], 1)], 1)
    c["c_rot"] = np.ascontiguousarray(np.tile(rot, (2, 1, 1, 1)), dtype=f32)
    c["c_heads8"] = (t[:, None] // SD == np.arange(HEADS)[None, :]).astype(f32)
    return c


def kernel(**inputs):
    import concourse.bacc as bacc
    from concourse.bass_utils import run_bass_kernel_spmd as run

    a = {k: np.asarray(v) for k, v in inputs.items()}
    arrays = dict(
        x=a["x"], ctx_in=a["ctx_1024"], mask=a["mask_BxS2_bk0"].reshape(1, -1).view(np.int32),
        params=a["L0_attn_params"], wvT=a["L0_attn_Wv"].T, bv=a["L0_attn_bv"].reshape(1, -1),
        woT_a=a["L0_attn_Wo"].T, bo=a["L0_attn_bo"].reshape(1, -1),
        wq=a["L0_xattn_W_Q"], wk=a["L0_xattn_W_K"], wv=a["L0_xattn_W_V"], wo_x=a["L0_xattn_W_O"],
        wqkv=a["L0_ffn_Wqkv"], q_scale=a["L0_ffn_q_scale"], k_scale=a["L0_ffn_k_scale"], wo=a["L0_ffn_Wo"],
        ln_gT=a["L0_ffn_ln_g"].T, ln_bT=a["L0_ffn_ln_b"].T, w1=a["L0_ffn_W1"], b1T=a["L0_ffn_b1"].T,
        w2=a["L0_ffn_W2"], b2=a["L0_ffn_b2"], **constants())
    nc = bacc.Bacc("TRN2", target_bir_lowering=False, num_devices=1)
    feeds, aps = {}, []
    for name, v in arrays.items():
        v = np.ascontiguousarray(v)
        feeds["in_" + name] = v
        aps.append(nc.dram_tensor("in_" + name, v.shape, mybir.dt.from_np(v.dtype), kind="ExternalInput").ap())
    aps.append(nc.dram_tensor("out_0", (BATCH, SEQ, DIM), FP32, kind="ExternalOutput").ap())
    build(nc, *aps)
    r = run(nc, [feeds], core_ids=[0])
    return r.results[0]["out_0"]
```

```python
import numpy as np
from contextlib import ExitStack

import concourse.bass as bass
from concourse import mybir

FP32, BF16, I32, U8 = mybir.dt.float32, mybir.dt.bfloat16, mybir.dt.int32, mybir.dt.uint8
ALU = mybir.AluOpType
ACT = mybir.ActivationFunctionType
AX = mybir.AxisListType

BATCH, SEQ, DIM = 64, 64, 128
TILES = BATCH * SEQ // 128
HEADS, PAIRS = 16, 8
HD = 64
SD = DIM // HEADS
DEPTH, WINDOW = 6, 32
INNER = HEADS * HD
FF = int(DIM * 4 * 2 / 3)
FF_CHUNKS = [(c * 128, min(128, FF - c * 128)) for c in range(3)]
MASKED = -1.0e37
RSQRT_MAGIC = float(0x5F3759DF)
EPS = 1e-5


class Names:
    pass


def at_least(eng, sem, value):
    if not isinstance(value, int) or value > 0:
        eng.wait_ge(sem, value)


def hold(eng, held):
    eng.sem_inc(held, 1)


def run_pipeline(eng, turn, tiles):
    turn(-1, 1, True, False, False, False)
    turn(0, 0, True, True, False, False)
    turn(1, 1, True, True, True, False)
    turn(2, 0, True, True, True, True)
    turn(3, 1, True, True, True, True)
    with eng.Fori(4, tiles - 3, 2) as i:
        turn(i, 0, True, True, True, True)
        turn(i + 1, 1, True, True, True, True)
    turn(tiles - 2, 0, True, True, True, True)
    turn(tiles - 1, 1, False, True, True, True)
    turn(tiles, 0, False, False, True, True)
    turn(tiles + 1, 1, False, False, False, True)
    turn(tiles + 2, 0, False, False, False, False)


def second_half(i, par):
    return par == 0 and (not isinstance(i, int) or i >= 4)


def flat(ap):
    return ap.rearrange("p a b -> p (a b)")


def build(nc, x, ctx_in, mask, params, wvT, bv, woT_a, bo, wq, wk, wv, wo_x, wqkv, q_scale, k_scale, wo,
          ln_gT, ln_bT, w1, b1T, w2, b2, c_ident, c_shift, c_causal, c_rot, c_heads8, out):
    es = ExitStack()
    with es:
        def sb(name, shape, dt=FP32):
            return es.enter_context(nc.sbuf_tensor(name, shape, dt))

        def sem(name):
            return es.enter_context(nc.semaphore(name))

        m = Names()
        m.x, m.ctx_in, m.mask, m.params, m.wvT, m.bv = x, ctx_in, mask, params, wvT, bv
        m.woT_a, m.bo, m.wq, m.wk, m.wv, m.wo_x = woT_a, bo, wq, wk, wv, wo_x
        m.wqkv, m.q_scale, m.k_scale, m.wo, m.ln_gT, m.ln_bT = wqkv, q_scale, k_scale, wo, ln_gT, ln_bT
        m.w1, m.b1T, m.w2, m.b2, m.c_ident, m.c_shift = w1, b1T, w2, b2, c_ident, c_shift
        m.c_causal, m.c_rot, m.c_heads8, m.out = c_causal, c_rot, c_heads8, out

        m.X = sb("X", [128, TILES, DIM])
        m.Y = sb("Y", [128, TILES, DIM])
        m.WA = sb("WA", [128, 3 * INNER])
        m.WO = sb("WO", [128, PAIRS * DIM])
        m.W1 = sb("W1", [128, 2 * FF])
        m.W2 = sb("W2", [128, 3 * DIM])
        m.ident = sb("ident", [128, 128])
        m.identb = sb("identb", [128, 128], BF16)
        m.shift = sb("shift", [128, 128])
        m.causal = sb("causal", [128, 512])
        m.causalb = sb("causalb", [128, 512], BF16)
        m.rot = sb("rot", [128, 2, 2, HD])
        m.scales = sb("scales", [128, 2, 2, DEPTH, HD])
        m.tables = sb("tables", [128, DEPTH, 2, 2, HD])
        m.heads8 = sb("heads8", [128, HEADS])
        m.gcol = sb("gcol", [128, DEPTH])
        m.bcol = sb("bcol", [128, DEPTH])
        m.b1col = sb("b1col", [128, 2, 3, DEPTH])
        m.ones = sb("ones", [1, 128])
        m.onesb = sb("onesb", [1, 128], BF16)
        m.minus_half = sb("minus_half", [128, 1])
        m.bvrow = sb("bvrow", [1, DIM])
        m.borow = sb("borow", [1, DIM])
        m.tril = sb("tril", [128, SD])
        m.trilbd = sb("trilbd", [128, 128])
        m.trilT = sb("trilT", [128, 128])
        m.wqk = sb("wqk", [128, 128])
        m.wvT_sb = sb("wvT_sb", [128, 128])
        m.woT_sb = sb("woT_sb", [128, 128])
        m.mask8 = sb("mask8", [1, BATCH * SEQ // 4], I32)
        m.maskb = sb("maskb", [1, BATCH * SEQ], BF16)
        m.maskrow = sb("maskrow", [1, 2, 4, 128], BF16)
        m.ctx_sb = sb("ctx_sb", [128, 2, DIM])
        m.ystat = sb("ystat", [128, DIM])
        m.xsT = sb("xsT", [128, 2, SEQ])
        m.xsT_shifted = sb("xsT_shifted", [128, 2, SEQ])
        m.ctxT = sb("ctxT", [128, 128])
        m.sq = sb("sq", [128, 2048])
        m.ss = sb("ss", [128, 32])
        m.ssm = sb("ssm", [128, 32])
        m.bits = sb("bits", [128, 32], I32)
        m.seed = sb("seed", [128, 32], I32)
        m.rn = sb("rn", [128, 32])
        m.rn_a = sb("rn_a", [128, 32])
        m.rn_b = sb("rn_b", [128, 32])
        m.qn = sb("qn", [128, 2048])
        m.RA = sb("RA", [128, 2048])
        m.RB = sb("RB", [128, 2048])
        m.qTbd = sb("qTbd", [128, PAIRS, 2, 2, SEQ])
        m.kT = sb("kT", [128, PAIRS * 128])
        m.V = sb("V", [128, 2, HEADS * HD])
        m.D = sb("D", [128, 1024])
        m.P = sb("P", [128, 1024])
        m.mx = sb("mx", [128, 16])
        m.PTbd = sb("PTbd", [128, HEADS, 2, SEQ])
        m.row_sum = sb("row_sum", [128, 16])
        m.inv_sum = sb("inv_sum", [128, 16])
        m.OT = sb("OT", [128, PAIRS * 128])
        m.y1 = sb("y1", [128, 2, DIM])
        m.ys = sb("ys", [128, DIM])
        m.stats = sb("stats", [128, 6])
        m.mv = sb("mv", [128, 2])
        m.vare = sb("vare", [128, 1])
        m.rstd = sb("rstd", [128, 1])
        m.xn = sb("xn", [128, DIM])
        m.xnT = sb("xnT", [128, 2, 128])
        m.G = sb("G", [128, 3, 256])
        m.H = sb("H", [128, 3, 256])
        m.bank = [es.enter_context(nc.psum_tensor(f"bank{n}", [128, 512], FP32)) for n in range(8)]

        m.cross_w = sem("cross_weights")

        setup(nc, sem, m)
        for kind in ("self", "cross", "local"):
            stage(nc, sem, kind, m)
        finish(nc, sem, m)


def setup(nc, sem, m):
    dma, dmac = sem("setup_dma"), sem("setup_tril_zero")
    cast, zeroed, made = sem("setup_cast"), sem("setup_zeroed"), sem("setup_made")
    tril_done, tril_copied, norm = sem("setup_tril_done"), sem("setup_tril_copied"), sem("setup_norm")
    held = sem("setup_held")
    var, rstd_done, small = sem("setup_var"), sem("setup_rstd"), sem("setup_small")
    loads = [
        (m.X[:, :, :], m.x.rearrange("(t b) s d -> (b s) t d", b=2)),
        (m.ident[:, :], m.c_ident), (m.shift[:, :], m.c_shift), (m.causal[:, :], m.c_causal),
        (m.rot[:, :, :, :], m.c_rot), (m.heads8[:, :], m.c_heads8),
        (m.gcol[:, :], m.ln_gT), (m.bcol[:, :], m.ln_bT), (m.bvrow[:, :], m.bv), (m.borow[:, :], m.bo),
        (m.wvT_sb[:, :], m.wvT), (m.woT_sb[:, :], m.woT_a), (m.mask8[:, :], m.mask),
    ]
    for side in range(2):
        for c, (at, rows) in enumerate(FF_CHUNKS):
            loads.append((m.b1col[0:rows, side, c, :], m.b1T[side * FF + at:side * FF + at + rows, :]))
    half = HD // 2
    for n, s in enumerate((m.q_scale, m.k_scale)):
        wide = s.rearrange("l (a d) -> a l d", a=1)
        loads.append((m.scales[:, n, 0, :, :], wide.to_broadcast([128, DEPTH, HD])))
        for to, frm in ((0, half), (half, 0)):
            loads.append((m.scales[:, n, 1, :, to:to + half],
                          wide[:, :, frm:frm + half].to_broadcast([128, DEPTH, half])))
    with nc.Block() as block:

        @block.sync
        def _(sp):
            for dst, src in loads:
                sp.dma_start(dst, src).then_inc(dma, 16)
            sp.wait_ge(dmac, 1)
            for i in range(SD):
                off = i * (i + 1) // 2
                sp.dma_start(m.tril[i:128:SD, 0:i + 1], m.params[:, off:off + i + 1],
                             allow_slow_non_contiguous=True).then_inc(tril_done, 16)

        @block.gpsimd
        def _(pool):
            pool.memset(m.tril[:, :], 0.0).then_inc(dmac, 1)
            pool.memset(m.ones[:, :], 1.0)
            pool.memset(m.onesb[:, :], 1.0)
            pool.memset(m.minus_half[:, :], -0.5).then_inc(zeroed, 1)
            pool.memset(m.qTbd[:, :, :, :, :], 0.0)
            pool.memset(m.PTbd[:, :, :, :], 0.0)
            pool.memset(m.H[:, :, :], 1.0)
            pool.memset(m.qn[:, :], 0.0)
            pool.memset(m.RB[:, :], 0.0)
            pool.memset(m.xsT_shifted[:, :, :], 0.0)

            def inverse_root(t):
                at_least(pool, rstd_done, t)
                pool.wait_ge(var, t + 1)
                hold(pool, held)
                pool.tensor_scalar(m.vare[:, :], m.mv[:, 1:2], EPS, None, ALU.add).then_inc(small, 1)
                pool.wait_ge(small, t + 1)
                pool.tensor_tensor(m.rstd[:, :], m.vare[:, :], m.minus_half[:, :], ALU.pow).then_inc(rstd_done, 1)

            inverse_root(0)
            with pool.Fori(1, TILES, 1) as t:
                inverse_root(t)

        @block.vector
        def _(dve):
            dve.wait_ge(dma, 16 * len(loads))
            dve.tensor_copy(m.identb[:, :], m.ident[:, :]).then_inc(cast, 1)
            dve.tensor_copy(m.causalb[:, :], m.causal[:, :]).then_inc(cast, 1)
            dve.tensor_scalar(m.maskb[:, :], m.mask8[:, :].bitcast(U8), MASKED, None, ALU.mult).then_inc(cast, 1)
            for n in range(2):
                for s in range(2):
                    dve.tensor_tensor(m.tables[:, :, n, s, :], m.scales[:, n, s, :, :],
                                      m.rot[:, n, s, :].unsqueeze(1).to_broadcast([128, DEPTH, HD]), ALU.mult)
            dve.wait_ge(tril_done, 16 * SD)
            dve.tensor_tensor(m.trilbd[:, :].rearrange("p (h j) -> p h j", j=SD),
                              m.tril[:, :].unsqueeze(1).to_broadcast([128, HEADS, SD]),
                              m.heads8[:, :].unsqueeze(2).to_broadcast([128, HEADS, SD]), ALU.mult).then_inc(made, 1)

            def normalise(t):
                at_least(dve, norm, t)
                hold(dve, held)
                dve.bn_stats(m.stats[:, :], m.X[:, bass.ds(t, 1), :]).then_inc(cast, 1)
                dve.wait_ge(cast, t + 4)
                hold(dve, held)
                dve.bn_aggr(m.mv[:, :], m.stats[:, :]).then_inc(var, 1)
                dve.wait_ge(rstd_done, t + 1)
                dve.tensor_scalar(m.Y[:, bass.ds(t, 1), :], m.X[:, bass.ds(t, 1), :], m.mv[:, 0:1], m.rstd[:, 0:1],
                                  ALU.subtract, ALU.mult).then_inc(norm, 1)

            normalise(0)
            with dve.Fori(1, TILES, 1) as t:
                normalise(t)

        @block.tensor
        def _(pe):
            pe.wait_ge(made, 1)
            pe.transpose(m.bank[0][:, 0:128], m.trilbd[:, :], m.ident[:, :]).then_inc(tril_copied, 1)
            pe.wait_ge(made, 2)
            pe.matmul(m.bank[1][:, 0:128], m.trilT[:, :], m.trilT[:, :], start=True, stop=True).then_inc(tril_copied, 1)

        @block.scalar
        def _(act):
            act.wait_ge(tril_copied, 1)
            act.activation(m.trilT[:, :], m.bank[0][:, 0:128], ACT.Copy).then_inc(made, 1)
            act.wait_ge(tril_copied, 2)
            act.activation(m.wqk[:, :], m.bank[1][:, 0:128], ACT.Copy).then_inc(made, 1)


def finish(nc, sem, m):
    summed, stored = sem("finish_summed"), sem("finish_stored")
    parts = 4
    n = TILES // parts
    out = m.out.rearrange("(t b) s d -> (b s) t d", b=2)
    with nc.Block() as block:

        @block.vector
        def _(dve):
            for c in range(parts):
                part = slice(c * n, (c + 1) * n)
                dve.tensor_tensor(m.X[:, part, :], m.X[:, part, :], m.Y[:, part, :], ALU.add).then_inc(summed, 1)

        @block.sync
        def _(sp):
            for c in range(parts):
                part = slice(c * n, (c + 1) * n)
                sp.wait_ge(summed, c + 1)
                sp.dma_start(out[:, part, :], m.X[:, part, :]).then_inc(stored, 16)
            sp.wait_ge(stored, 16 * parts)


def stage(nc, sem, kind, m):
    SELF, CROSS, LOCAL = kind == "self", kind == "cross", kind == "local"
    N = TILES * DEPTH if LOCAL else TILES
    DV = SD if SELF else HD
    EXP_SCALE = {"self": SD ** -0.5, "cross": HD ** -0.5, "local": 8.0}[kind]
    NPRE = 1 if SELF else 2
    NQK = 1 if SELF else 4
    NQT, NKT = (2, 1) if SELF else (4, 2)
    NV = NO = 1 if SELF else 2
    NRN = 12
    b = m.bank
    s = Names()
    s.w_in = sem(f"{kind}_w_in")
    s.w_out = sem(f"{kind}_w_out")
    s.ystat = sem(f"{kind}_ystat")
    s.pre_t = sem(f"{kind}_pre_t")
    s.pre_copied = sem(f"{kind}_pre_copied")
    s.qk = sem(f"{kind}_qk")
    s.qT = sem(f"{kind}_qT")
    s.kT = sem(f"{kind}_kT")
    s.v = sem(f"{kind}_v")
    s.v_copied = sem(f"{kind}_v_copied")
    s.scores = sem(f"{kind}_scores")
    s.mx = sem(f"{kind}_mx")
    s.diff = sem(f"{kind}_diff")
    s.probs = sem(f"{kind}_probs")
    s.pt = sem(f"{kind}_pt")
    s.pt_copied = sem(f"{kind}_pt_copied")
    s.o = sem(f"{kind}_o")
    s.row_sum = sem(f"{kind}_row_sum")
    s.pnorm = sem(f"{kind}_pnorm")
    s.recip = sem(f"{kind}_recip")
    s.ot_copied = sem(f"{kind}_ot_copied")
    s.wo = sem(f"{kind}_wo")
    s.y1 = sem(f"{kind}_y1")
    s.stats = sem(f"{kind}_stats")
    s.var = sem(f"{kind}_var")
    s.vare = sem(f"{kind}_vare")
    s.rstd = sem(f"{kind}_rstd")
    s.xn = sem(f"{kind}_xn")
    if CROSS:
        s.ctx_even = sem(f"{kind}_ctx_even")
        s.ctx_odd = sem(f"{kind}_ctx_odd")
        s.mask_made = sem(f"{kind}_mask_made")
    if LOCAL:
        s.w_ff = sem(f"{kind}_w_ff")
        s.sq = sem(f"{kind}_sq")
        s.ss = sem(f"{kind}_ss")
        s.seed = sem(f"{kind}_seed")
        s.newton = sem(f"{kind}_newton")
        s.qn = sem(f"{kind}_qn")
        s.ra = sem(f"{kind}_ra")
        s.half = sem(f"{kind}_half")
        s.rotated = sem(f"{kind}_rotated")
        s.rot = sem(f"{kind}_rot")
        s.sh = sem(f"{kind}_sh")
        s.sh_copied = sem(f"{kind}_sh_copied")
        s.ys = sem(f"{kind}_ys")
        s.xn_t = sem(f"{kind}_xn_t")
        s.xn_copied = sem(f"{kind}_xn_copied")
        s.ff = sem(f"{kind}_ff")
        s.gelu = sem(f"{kind}_gelu")
        s.h = sem(f"{kind}_h")
        s.w2 = sem(f"{kind}_w2")
        s.y = sem(f"{kind}_y")
    held = sem(f"{kind}_held")
    V = [m.qn[:, :], m.RB[:, :]] if SELF else [m.V[:, 0, :], m.V[:, 1, :]]
    qTbd = m.RA[:, :].rearrange("p (h t a q) -> p h t a q", h=PAIRS, t=2, a=2) if SELF else m.qTbd
    xsT_tokens = m.xsT_shifted if LOCAL else m.xsT
    xsT = flat(xsT_tokens[:, :, :])

    def slot(t):
        return t % TILES if LOCAL else t

    def tile_of(buf, t):
        return flat(buf[:, bass.ds(slot(t), 1), :])

    with nc.Block() as block:

        @block.sync
        def _(sp):
            if SELF:
                for c, w in enumerate((m.wq, m.wk, m.wv)):
                    sp.dma_start(m.WA[:, c * INNER:(c + 1) * INNER], w).then_inc(m.cross_w, 16)
                sp.dma_start(m.WO[:, :].rearrange("p (c n) -> p c n", n=DIM),
                             m.wo_x.rearrange("(c p) n -> p c n", p=128)).then_inc(m.cross_w, 16)
            if CROSS:
                ctx_tiles = m.ctx_in.rearrange("(t b) s d -> t (b s) d", b=2)

                def load_ctx(t, par):
                    at_least(sp, s.pre_t, t - 1)
                    sp.dma_start(m.ctx_sb[:, par, :], flat(ctx_tiles[bass.ds(t, 1), :, :].rearrange("a p d -> p a d")))\
                      .then_inc((s.ctx_even, s.ctx_odd)[par], 16)

                load_ctx(0, 0)
                load_ctx(1, 1)
                with sp.Fori(2, N - 1, 2) as t:
                    load_ctx(t, 0)
                    load_ctx(t + 1, 1)
            if LOCAL:
                def load_in(l):
                    sp.dma_start(m.WA[:, :], flat(m.wqkv[bass.ds(l, 1), :, :].rearrange("a p n -> p a n")))\
                      .then_inc(s.w_in, 16)

                def load_out(l):
                    sp.dma_start(m.WO[:, :].rearrange("p (c n) -> p c n", n=DIM),
                                 m.wo[bass.ds(l, 1), :, :].rearrange("a (c p) n -> p (a c) n", p=128)).then_inc(s.w_out, 16)

                def load_ff(l):
                    at, rows = FF_CHUNKS[2]
                    one = bass.ds(l, 1)
                    sp.dma_start(m.W1[:, :], flat(m.w1[one, :, :].rearrange("a p n -> p a n"))).then_inc(s.w_ff, 16)
                    sp.dma_start(m.W2[:, 0:2 * DIM].rearrange("p (c n) -> p c n", n=DIM),
                                 m.w2[one, 0:at, :].rearrange("a (c p) n -> p (a c) n", p=128)).then_inc(s.w_ff, 16)
                    sp.dma_start(m.W2[0:rows, 2 * DIM:3 * DIM],
                                 flat(m.w2[one, at:FF, :].rearrange("a p n -> p a n"))).then_inc(s.w_ff, 16)
                    sp.dma_start(m.W2[rows:rows + 1, 2 * DIM:3 * DIM], m.b2[one, :]).then_inc(s.w_ff, 16)

                load_in(0)
                load_out(0)
                load_ff(0)
                with sp.Fori(1, DEPTH, 1) as l:
                    sp.wait_ge(s.v, NV * TILES * l)
                    load_in(l)
                    sp.wait_ge(s.wo, TILES * l)
                    load_out(l)
                    sp.wait_ge(s.w2, TILES // 2 * l)
                    load_ff(l)

        @block.tensor
        def _(pe):
            mm = nc.tensor.matmul

            def out_projection(t):
                pe.wait_ge(s.ot_copied, NO * (t + 1))
                if SELF:
                    mm(b[4][:, 0:128], m.OT[:, 0:128], m.woT_sb[:, :], start=True, stop=False)
                    mm(b[4][:, 0:128], m.ones[:, :], m.borow[:, :], start=False, stop=True).then_inc(s.wo, 1)
                    return
                if LOCAL:
                    pe.wait_ge(s.w_out, 16 * (t // TILES) + 16)
                for c in range(PAIRS):
                    last = mm(b[4][:, 0:128], m.OT[:, c * 128:(c + 1) * 128], m.WO[:, c * 128:(c + 1) * 128],
                              start=(c == 0), stop=(c == PAIRS - 1))
                last.then_inc(s.wo, 1)

            def bank_copied(t, c):
                if c < 2:
                    at_least(pe, s.qT, NQT * (t - 1) + 2 * c + 2)
                else:
                    at_least(pe, s.kT, NKT * (t - 1) + c - 1)

            def queries_keys(t):
                pe.wait_ge(s.pre_copied, NPRE * (t + 1))
                if SELF:
                    at_least(pe, s.qT, NQT * t)
                    mm(b[0][:, 0:128], m.wqk[:, :], xsT, start=True, stop=True).then_inc(s.qk, 1)
                if CROSS:
                    if isinstance(t, int) and t == 0:
                        pe.wait_ge(m.cross_w, 64)
                    for c in range(4):
                        bank_copied(t, c)
                        for n in range(4):
                            at = c * 512 + n * 128
                            last = mm(b[c][:, n * 128:(n + 1) * 128], m.WA[:, at:at + 128],
                                      xsT if c < 2 else m.ctxT[:, :], start=True, stop=True)
                        last.then_inc(s.qk, 1)
                if LOCAL:
                    pe.wait_ge(s.w_in, 16 * (t // TILES) + 16)
                    for c in range(4):
                        bank_copied(t, c)
                        mm(b[c][:, :], xsT, m.WA[:, c * 512:(c + 1) * 512], start=True, stop=True).then_inc(s.qk, 1)

            def values(t, c):
                if SELF:
                    mm(b[6][:, 0:128], xsT, m.wvT_sb[:, :], start=True, stop=False)
                    mm(b[6][:, 0:128], m.ones[:, :], m.bvrow[:, :], start=False, stop=True).then_inc(s.v, 1)
                    return
                at = 2 * INNER + c * 512
                mm(b[6 + c][:, :], xsT if LOCAL else m.ctxT[:, :], m.WA[:, at:at + 512],
                   start=True, stop=True).then_inc(s.v, 1)

            def scores(t, par):
                pe.wait_ge(s.qT, NQT * (t + 1))
                pe.wait_ge(s.kT, NKT * (t + 1))
                at_least(pe, s.pt_copied, 4 * t)
                if CROSS:
                    pe.wait_ge(s.mask_made, t + 1)
                for j in range(2):
                    if CROSS:
                        mm(b[4 + j][:, :], m.onesb[:, :], m.maskrow[:, par, :, :].rearrange("p a k -> p (a k)"),
                           start=True, stop=False)
                    if LOCAL:
                        mm(b[4 + j][:, :], m.identb[:, :], m.causalb[:, :], start=True, stop=False)
                    for n in range(8):
                        hp, bb = 4 * j + n // 2, n % 2
                        keys = bb * 64 if SELF else hp * 128 + bb * 64
                        last = mm(b[4 + j][:, n * 64:(n + 1) * 64], flat(qTbd[:, hp, bb, :, :]),
                                  m.kT[:, keys:keys + 64], start=SELF, stop=SELF or n == 7)
                    last.then_inc(s.scores, 1)

            def probs_transposed(t, j):
                pe.wait_ge(s.pnorm, 2 * t + j + 1)
                for n in range(4):
                    c = 4 * j + n
                    last = nc.tensor.transpose(b[4 + j][:, n * 128:(n + 1) * 128], m.P[:, c * 128:(c + 1) * 128],
                                               m.ident[:, :])
                last.then_inc(s.pt, 1)

            def rotated_transposed(t, j):
                pe.wait_ge(s.qn, 4 * t + j + 1)
                for n in range(4):
                    at, col = j * 512 + n * 128, n * 128
                    last = nc.tensor.transpose(b[j][:, col:col + 128], m.qn[:, at:at + 128], m.ident[:, :])
                last.then_inc(s.rot, 1)

            def head_outputs(t, par):
                pe.wait_ge(s.v_copied, NV * (t + 1))
                pe.wait_ge(s.pt_copied, 4 * (t + 1))
                for h in range(HEADS):
                    probs = flat(m.PTbd[:, h, :, :])
                    if SELF:
                        last = mm(b[6][:, 0:128], V[par][:, h * DIM:(h + 1) * DIM], probs,
                                  start=(h == 0), stop=(h == HEADS - 1))
                        continue
                    rows, col = slice(HD * (h % 2), HD * (h % 2) + HD), h // 2 % 4 * 128
                    last = mm(b[6 + h // 8][rows, col:col + 128], V[par][:, h * HD:(h + 1) * HD], probs,
                              start=True, stop=True)
                    if h == 7:
                        last.then_inc(s.o, 1)
                last.then_inc(s.o, 1)

            def pre_transposed(t, par):
                pe.wait_ge(s.ystat, t + 1)
                last = nc.tensor.transpose(b[6][:, 0:128], m.ystat[:, :], m.ident[:, :])
                if CROSS:
                    pe.wait_ge((s.ctx_even, s.ctx_odd)[par], 16 * ((t - par) // 2) + 16)
                    last = nc.tensor.transpose(b[6][:, 128:256], m.ctx_sb[:, par, :], m.ident[:, :])
                last.then_inc(s.pre_t, 1)

            def feed_forward_in(t, c):
                pe.wait_ge(s.w_ff, 64 * (t // TILES) + 64)
                at, rows = FF_CHUNKS[c]
                bk = b[7 - c % 2]
                if c == 2:
                    pe.wait_ge(s.h, 3 * ((t - 1) // 2) + 1)
                for side, off in ((0, FF), (1, 0)):
                    last = mm(bk[0:rows, side * 256:(side + 1) * 256], m.W1[:, off + at:off + at + rows],
                              flat(m.xnT[:, :, :]), start=True, stop=True)
                last.then_inc(s.ff, 1)

            def feed_forward_out(t):
                pe.wait_ge(s.h, 3 * ((t - 1) // 2) + 3)
                for n in range(2):
                    for c, (_, rows) in enumerate(FF_CHUNKS):
                        k = rows + (c == 2)
                        last = mm(b[6][:, n * 128:(n + 1) * 128], m.H[0:k, c, n * 128:(n + 1) * 128],
                                  m.W2[0:k, c * 128:(c + 1) * 128], start=(c == 0), stop=(c == 2))
                last.then_inc(s.w2, 1)

            def outputs_banks_free(i, par):
                static = isinstance(i, int)
                pe.wait_ge(s.v_copied, NV * (min(i, N) if static else i))
                pe.wait_ge(s.pre_copied, NPRE * (min(i + 1, N) if static else i + 1))
                if LOCAL:
                    at_least(pe, s.xn_copied, i - 2)
                    if par == 0:
                        pe.wait_ge(s.y, TILES // 2 + (i - 2) // 2)

            def turn(i, par, pre, head, mid, tail):
                late = LOCAL and second_half(i, par)
                outputs_last = late or not LOCAL
                if head:
                    queries_keys(i)
                if late:
                    feed_forward_in(i - 3, 2)
                if tail and not outputs_last:
                    outputs_banks_free(i, par)
                    head_outputs(i - 2, par)
                if mid:
                    scores(i - 1, 1 - par)
                if late:
                    feed_forward_out(i - 3)
                if tail and outputs_last:
                    outputs_banks_free(i, par)
                    head_outputs(i - 2, par)
                if late and head:
                    rotated_transposed(i, 0)
                if tail:
                    if mid:
                        pe.wait_ge(s.diff, 2 * (i - 1) + 1)
                    out_projection(i - 2)
                if head:
                    for j in range(NV):
                        values(i, j)
                if head and LOCAL:
                    for j in range(late, 3):
                        rotated_transposed(i, j)
                if tail and LOCAL:
                    pe.wait_ge(s.y1, i - 1)
                    pe.wait_ge(s.ys, i - 1)
                    mm(b[4][:, 128:192], m.shift[:, :], m.y1[:, par, 64:128], start=True, stop=True).then_inc(s.sh, 1)
                if head and LOCAL:
                    rotated_transposed(i, 3)
                if pre:
                    if head:
                        pe.wait_ge(s.v_copied, NV * i + 1)
                    pre_transposed(i + 1, 1 - par)
                if mid:
                    if tail:
                        pe.wait_ge(s.sh_copied if LOCAL else s.y1, i - 1)
                    probs_transposed(i - 1, 0)
                    probs_transposed(i - 1, 1)
                if tail and LOCAL:
                    pe.wait_ge(s.xn, i - 1)
                    if head:
                        pe.wait_ge(s.v_copied, NV * (i + 1))
                    if pre:
                        pe.wait_ge(s.pre_copied, NPRE * (i + 2))
                    nc.tensor.transpose(b[6][:, 0:128], m.xn[:, :], m.ident[:, :]).then_inc(s.xn_t, 1)
                if tail and LOCAL and par == 1:
                    pe.wait_ge(s.xn_copied, i - 1)
                    feed_forward_in(i - 2, 0)
                    feed_forward_in(i - 2, 1)

            run_pipeline(pe, turn, N)

        @block.scalar
        def _(act):
            def copy(dst, src):
                return nc.scalar.activation(dst, src, ACT.Copy)

            def values_out(i, par, j):
                act.wait_ge(s.v, NV * i + j + 1)
                if SELF:
                    blocks = V[par][:, 0:HEADS * DIM].rearrange("p (h g d) -> p h g d", h=HEADS, d=SD)
                    for h in range(HEADS):
                        last = copy(blocks[:, h, h, :], b[6][:, h * SD:(h + 1) * SD])
                    last.then_inc(s.v_copied, 1)
                else:
                    copy(V[par][:, j * 512:(j + 1) * 512], b[6 + j][:, :]).then_inc(s.v_copied, 1)

            def probs_out(t, j):
                act.wait_ge(s.pt, 2 * t + j + 1)
                for bb in range(2):
                    rows = slice(64 * bb, 64 * bb + 64)
                    copy(m.PTbd[rows, 8 * j:8 * j + 8, bb, :],
                         b[4 + j][rows, :].rearrange("p (h q) -> p h q", q=SEQ)).then_inc(s.pt_copied, 1)

            def gates(t, c):
                act.wait_ge(s.ff, 3 * ((t - 1) // 2) + c + 1)
                rows = FF_CHUNKS[c][1]
                nc.scalar.activation(m.G[0:rows, c, :], b[7 - c % 2][0:rows, 0:256], ACT.Gelu,
                                     bias=m.b1col[0:rows, 1, c, bass.ds(t // TILES, 1)]).then_inc(s.gelu, 1)

            def queries_out(i, ready, j):
                at_least(act, s.scores, 2 * i)
                act.wait_ge(ready, 4 * i + j + 1)
                for a in range(2):
                    rows = slice(64 * a, 64 * a + 64)
                    copy(qTbd[rows, 4 * j:4 * j + 4, :, a, :],
                         b[j][rows, :].rearrange("p (h t q) -> p h t q", h=4, q=SEQ)).then_inc(s.qT, 1)

            def outputs_out(i):
                for j in range(NO):
                    act.wait_ge(s.o, NO * (i - 2) + j + 1)
                    n = 128 if SELF else 512
                    copy(m.OT[:, j * n:(j + 1) * n], b[6 + j][:, 0:n]).then_inc(s.ot_copied, 1)

            def keys_out(i, ready, j):
                act.wait_ge(ready, 4 * i + 2 + j + 1)
                copy(m.kT[:, j * 512:(j + 1) * 512], b[2 + j][:, :]).then_inc(s.kT, 1)

            def turn(i, par, pre, head, mid, tail):
                late = LOCAL and second_half(i, par)
                outputs_last = late or not LOCAL
                ready = s.rot if LOCAL else s.qk
                if head and LOCAL:
                    for j in range(4):
                        act.wait_ge(s.qk, 4 * i + j + 1)
                        at_least(act, s.ss, 4 * (i - 1) + j + 1)
                        nc.scalar.activation(m.sq[:, j * 512:(j + 1) * 512], b[j][:, :], ACT.Square).then_inc(s.sq, 1)
                if late:
                    gates(i - 3, 2)
                if tail and not outputs_last:
                    outputs_out(i)
                if mid:
                    for j in range(2):
                        act.wait_ge(s.diff, 2 * (i - 1) + j + 1)
                        nc.scalar.activation(m.P[:, j * 512:(j + 1) * 512], m.D[:, j * 512:(j + 1) * 512], ACT.Exp,
                                             scale=EXP_SCALE).then_inc(s.probs, 1)
                if tail and outputs_last:
                    outputs_out(i)
                if head and SELF:
                    at_least(act, s.scores, 2 * i)
                    act.wait_ge(s.pre_copied, i + 1)
                    copy(m.kT[:, 0:128], xsT).then_inc(s.kT, 1)
                early = late or CROSS
                if early and head:
                    queries_out(i, ready, 0)
                if head:
                    for j in range(NV):
                        values_out(i, par, j)
                if head and not SELF:
                    for j in range(early, 2):
                        queries_out(i, ready, j)
                    keys_out(i, ready, 0)
                if tail and LOCAL:
                    act.wait_ge(s.sh, i - 1)
                    at_least(act, s.xn, i - 2)
                    copy(m.ys[:, 64:128], b[4][:, 128:192]).then_inc(s.sh_copied, 1)
                if head and not SELF:
                    keys_out(i, ready, 1)
                if pre:
                    act.wait_ge(s.pre_t, i + 2)
                    if SELF:
                        at_least(act, s.kT, i + 1)
                    if LOCAL:
                        copy(xsT_tokens[0:64, :, :], b[6][0:64, 0:128].rearrange("p (a q) -> p a q", q=SEQ))\
                            .then_inc(s.pre_copied, 1)
                        copy(xsT_tokens[64:128, :, 1:SEQ], b[6][64:128, 0:128].rearrange("p (a q) -> p a q", q=SEQ)[:, :, 0:SEQ - 1])\
                            .then_inc(s.pre_copied, 1)
                    else:
                        copy(xsT, b[6][:, 0:128]).then_inc(s.pre_copied, 1)
                    if CROSS:
                        copy(m.ctxT[:, :], b[6][:, 128:256]).then_inc(s.pre_copied, 1)
                if mid:
                    probs_out(i - 1, 0)
                    probs_out(i - 1, 1)
                if tail and LOCAL:
                    act.wait_ge(s.xn_t, i - 1)
                    l = (i - 2) // TILES
                    nc.scalar.activation(m.xnT[:, par, :], b[6][:, 0:128], ACT.Identity, scale=m.gcol[:, bass.ds(l, 1)],
                                         bias=m.bcol[:, bass.ds(l, 1)]).then_inc(s.xn_copied, 1)
                if tail and LOCAL and par == 1:
                    at_least(act, s.h, 3 * ((i - 3) // 2))
                    gates(i - 2, 0)
                    gates(i - 2, 1)

            run_pipeline(act, turn, N)

        @block.vector
        def _(dve):
            tt = nc.vector.tensor_tensor

            def chunk(buf, j):
                return buf[:, j * 512:(j + 1) * 512].rearrange("p (h d) -> p h d", d=HD)

            def squares_summed(i, j):
                dve.wait_ge(s.sq, 4 * i + j + 1)
                nc.vector.tensor_reduce(m.ss[:, 8 * j:8 * j + 8], chunk(m.sq, j), AX.X, ALU.add).then_inc(s.ss, 1)

            def cosine_part(i, j):
                dve.wait_ge(s.qk, 4 * i + j + 1)
                at_least(dve, s.rotated, 4 * (i - 1) + j + 1)
                tab = m.tables[:, bass.ds(i // TILES, 1), j // 2, 0, :].to_broadcast([128, 8, HD])
                tt(chunk(m.RA, j), b[j][:, :].rearrange("p (h d) -> p h d", d=HD), tab, ALU.mult).then_inc(s.ra, 1)

            def sine_part(i, j):
                half = HD // 2
                dve.wait_ge(s.qk, 4 * i + j + 1)
                at_least(dve, s.qn, 4 * (i - 1) + j + 1)
                src, dst = b[j][:, :].rearrange("p (h d) -> p h d", d=HD), chunk(m.RB, j)
                for to, frm in ((0, half), (half, 0)):
                    tab = m.tables[:, bass.ds(i // TILES, 1), j // 2, 1, to:to + half].to_broadcast([128, 8, half])
                    last = tt(dst[:, :, to:to + half], src[:, :, frm:frm + half], tab, ALU.mult)
                last.then_inc(s.half, 1)

            def over_length(i, j):
                dve.wait_ge(s.newton, NRN * (i + 1))
                dve.wait_ge(s.rotated, 4 * i + j + 1)
                at_least(dve, s.rot, 4 * (i - 1) + j + 1)
                tt(chunk(m.qn, j), chunk(m.RB, j), m.rn[:, 8 * j:8 * j + 8].unsqueeze(2).to_broadcast([128, 8, HD]),
                   ALU.mult).then_inc(s.qn, 1)

            def less_maximum(i, j):
                at_least(dve, s.diff, 2 * (i - 2) + j + 1)
                dve.wait_ge(s.scores, 2 * (i - 1) + j + 1)
                rows = b[4 + j][:, :].rearrange("p (n k) -> p n k", k=SEQ)
                nc.vector.tensor_reduce(m.mx[:, 8 * j:8 * j + 8], rows, AX.X, ALU.max).then_inc(s.mx, 1)
                dve.wait_ge(s.mx, 2 * (i - 1) + j + 1)
                tt(m.D[:, j * 512:(j + 1) * 512].rearrange("p (n k) -> p n k", k=SEQ), rows,
                   m.mx[:, 8 * j:8 * j + 8].unsqueeze(2).to_broadcast([128, 8, SEQ]), ALU.subtract)\
                    .then_inc(s.diff, 1)

            def row_sums(i, j):
                heads = slice(8 * j, 8 * j + 8)
                at_least(dve, s.recip, 2 * (i - 2) + j + 1)
                dve.wait_ge(s.probs, 2 * (i - 1) + j + 1)
                nc.vector.tensor_reduce(m.row_sum[:, heads], m.P[:, j * 512:(j + 1) * 512].rearrange("p (n k) -> p n k", k=SEQ),
                                        AX.X, ALU.add).then_inc(s.row_sum, 1)
                at_least(dve, s.pnorm, 2 * (i - 2) + j + 1)
                dve.wait_ge(s.row_sum, 2 * (i - 1) + j + 1)
                nc.vector.reciprocal(m.inv_sum[:, heads], m.row_sum[:, heads]).then_inc(s.recip, 1)

            def gated(t, c):
                rows = FF_CHUNKS[c][1]
                dve.wait_ge(s.gelu, 3 * ((t - 1) // 2) + c + 1)
                nc.vector.scalar_tensor_tensor(
                    out=m.H[0:rows, c, :], in0=b[7 - c % 2][0:rows, 256:512],
                    scalar=m.b1col[0:rows, 0, c, bass.ds(t // TILES, 1)],
                    in1=m.G[0:rows, c, :], op0=ALU.add, op1=ALU.mult).then_inc(s.h, 1)

            def statistics(i, row):
                at_least(dve, s.xn, i - 2)
                if LOCAL:
                    dve.wait_ge(s.sh_copied, i - 1)
                    dve.wait_ge(s.ys, i - 1)
                else:
                    dve.wait_ge(s.y1, i - 1)
                hold(dve, held)
                nc.vector.bn_stats(m.stats[:, :], row).then_inc(s.stats, 1)
                dve.wait_ge(s.stats, i - 1)
                hold(dve, held)
                nc.vector.bn_aggr(m.mv[:, :], m.stats[:, :]).then_inc(s.var, 1)

            def normalised(i, row):
                dve.wait_ge(s.rstd, i - 1)
                nc.vector.tensor_scalar(m.xn[:, :] if LOCAL else tile_of(m.Y, i - 2), row, m.mv[:, 0:1], m.rstd[:, 0:1],
                                        ALU.subtract, ALU.mult).then_inc(s.xn, 1)

            def turn(i, par, pre, head, mid, tail):
                late = LOCAL and second_half(i, par)
                outputs_last = late or not LOCAL
                rotary = head and LOCAL
                if rotary:
                    at_least(dve, s.seed, 3 * i)
                    squares_summed(i, 0)
                    cosine_part(i, 0)
                    squares_summed(i, 1)
                    sine_part(i, 0)
                    squares_summed(i, 2)
                    cosine_part(i, 1)
                    squares_summed(i, 3)
                    dve.wait_ge(s.ss, 4 * (i + 1))
                    at_least(dve, s.newton, NRN * i)
                    nc.vector.tensor_scalar(m.ssm[:, :], m.ss[:, :], 1e-24, None, ALU.max).then_inc(s.seed, 1)
                    dve.wait_ge(s.seed, 3 * i + 1)
                    nc.vector.tensor_scalar(m.bits[:, :], m.ssm[:, :].bitcast(I32), 1, None, ALU.arith_shift_right)\
                        .then_inc(s.seed, 1)
                    dve.wait_ge(s.seed, 3 * i + 2)
                    nc.vector.tensor_scalar(m.seed[:, :], m.bits[:, :], -1.0, RSQRT_MAGIC, ALU.mult, ALU.add)\
                        .then_inc(s.seed, 1)
                if late:
                    gated(i - 3, 2)
                if rotary:
                    sine_part(i, 1)
                    cosine_part(i, 2)
                if mid and late:
                    less_maximum(i, 0)
                if rotary:
                    sine_part(i, 2)
                if late:
                    dve.wait_ge(s.w2, (i - 4) // 2 + 1)
                    pairs = m.Y[:, :, :].rearrange("p (t a) d -> p t (a d)", a=2)
                    tt(flat(pairs[:, bass.ds((i - 4) // 2 % (TILES // 2), 1), :]), flat(m.y1[:, :, :]), b[6][:, 0:256],
                       ALU.add).then_inc(s.y, 1)
                if mid and not late:
                    less_maximum(i, 0)
                if rotary and late:
                    over_length(i, 0)
                if mid:
                    less_maximum(i, 1)
                if rotary:
                    cosine_part(i, 3)
                    sine_part(i, 3)
                if head and SELF:
                    dve.wait_ge(s.qk, i + 1)
                    at_least(dve, s.scores, 2 * i)
                    for bb in range(2):
                        tt(qTbd[:, :, bb, :, :],
                           b[0][:, bb * 64:(bb + 1) * 64].unsqueeze(1).unsqueeze(1).to_broadcast([128, PAIRS, 2, SEQ]),
                           m.heads8[:, :].rearrange("p (a c) -> p a c", c=2).unsqueeze(3).to_broadcast([128, PAIRS, 2, SEQ]),
                           ALU.mult).then_inc(s.qT, 1)
                if rotary and not late:
                    over_length(i, 0)
                if mid:
                    row_sums(i, 0)
                if rotary:
                    over_length(i, 1)
                if mid:
                    row_sums(i, 1)
                if rotary:
                    over_length(i, 2)
                if tail:
                    row = m.ys[:, :] if LOCAL else tile_of(m.X, i - 2)
                    if LOCAL:
                        dve.wait_ge(s.y, TILES // 2 + (i - 2) // 2)
                    dve.wait_ge(s.wo, i - 1)
                    src = tile_of(m.Y if LOCAL else m.X, i - 2)
                    dst = m.y1[:, par, :] if LOCAL else src
                    tt(dst, src, b[4][:, 0:128], ALU.add).then_inc(s.y1, 1)
                    if LOCAL:
                        at_least(dve, s.xn, i - 2)
                        tt(m.ys[:, 0:64], src[:, 0:64], b[4][:, 0:64], ALU.add).then_inc(s.ys, 1)
                if rotary:
                    over_length(i, 3)
                if tail:
                    statistics(i, row)
                    normalised(i, row)
                if tail and LOCAL and par == 1:
                    gated(i - 2, 0)
                    gated(i - 2, 1)

            if LOCAL:
                dve.sem_inc(s.y, TILES // 2)
            run_pipeline(dve, turn, N)

        @block.gpsimd
        def _(pool):
            tt = nc.gpsimd.tensor_tensor

            def inverse_deviation(i):
                at_least(pool, s.rstd, i - 2)
                pool.wait_ge(s.var, i - 1)
                hold(pool, held)
                nc.gpsimd.tensor_scalar(m.vare[:, :], m.mv[:, 1:2], EPS, None, ALU.add).then_inc(s.vare, 1)
                pool.wait_ge(s.vare, i - 1)
                tt(m.rstd[:, :], m.vare[:, :], m.minus_half[:, :], ALU.pow).then_inc(s.rstd, 1)

            def inverse_lengths(i):
                pool.wait_ge(s.seed, 3 * (i + 1))
                at_least(pool, s.newton, NRN * i)
                at_least(pool, s.qn, 4 * i)
                y = m.seed[:, :].bitcast(FP32)
                for step in range(3):
                    done = NRN * i + 4 * step
                    if step:
                        pool.wait_ge(s.newton, done)
                    tt(m.rn_a[:, :], y, y, ALU.mult).then_inc(s.newton, 1)
                    pool.wait_ge(s.newton, done + 1)
                    tt(m.rn_b[:, :], m.rn_a[:, :], m.ssm[:, :], ALU.mult).then_inc(s.newton, 1)
                    pool.wait_ge(s.newton, done + 2)
                    hold(pool, held)
                    nc.gpsimd.tensor_scalar(m.rn_a[:, :], m.rn_b[:, :], -0.5, 1.5, ALU.mult, ALU.add)\
                        .then_inc(s.newton, 1)
                    pool.wait_ge(s.newton, done + 3)
                    tt(m.rn[:, :], y, m.rn_a[:, :], ALU.mult).then_inc(s.newton, 1)
                    y = m.rn[:, :]

            def rotary_sum(i, j):
                at = slice(j * 512, (j + 1) * 512)
                pool.wait_ge(s.half, 4 * i + j + 1)
                pool.wait_ge(s.ra, 4 * i + j + 1)
                tt(m.RB[:, at], m.RB[:, at], m.RA[:, at], ALU.add).then_inc(s.rotated, 1)

            def normalised_probs(i, j):
                pool.wait_ge(s.recip, 2 * (i - 1) + j + 1)
                probs = m.P[:, j * 512:(j + 1) * 512].rearrange("p (n k) -> p n k", k=SEQ)
                tt(probs, probs, m.inv_sum[:, 8 * j:8 * j + 8].unsqueeze(2).to_broadcast([128, 8, SEQ]), ALU.mult)\
                    .then_inc(s.pnorm, 1)

            def turn(i, par, pre, head, mid, tail):
                if head and CROSS:
                    at_least(pool, s.scores, 2 * (i - 1))
                    hold(pool, held)
                    row = m.maskb[:, bass.ds(i * 128, 128)]
                    nc.gpsimd.tensor_copy(m.maskrow[:, par, :, :], row.unsqueeze(1).to_broadcast([1, 4, 128]))\
                        .then_inc(s.mask_made, 1)
                if head and LOCAL:
                    rotary_sum(i, 0)
                    inverse_lengths(i)
                    for j in range(1, 4):
                        rotary_sum(i, j)
                if pre:
                    if LOCAL:
                        pool.wait_ge(s.y, (i + 1) // 2 + 1)
                    at_least(pool, s.pre_t, i + 1)
                    hold(pool, held)
                    nc.gpsimd.tensor_copy(m.ystat[:, :], tile_of(m.Y, i + 1)).then_inc(s.ystat, 1)
                if mid:
                    normalised_probs(i, 0)
                    normalised_probs(i, 1)
                if tail:
                    inverse_deviation(i)

            run_pipeline(pool, turn, N)


def constants():
    f32 = np.float32
    c = {}
    c["c_ident"] = np.eye(128, dtype=f32)
    t = np.arange(128)
    c["c_shift"] = ((t[None, :] == t[:, None] + 1) & (t[None, :] % SEQ != 0)).astype(f32)
    q, k = t[:, None] % SEQ, np.arange(512)[None, :] % SEQ
    c["c_causal"] = np.where((k > q) | (q > k + WINDOW), f32(MASKED), f32(0))
    half = np.arange(0, HD, 2, dtype=f32)
    inv_freq = (1.0 / np.power(f32(10000.0), half / f32(HD))).astype(f32)
    pos = np.arange(SEQ, dtype=f32)
    freqs = np.tile(pos[:, None] * inv_freq[None, :], (1, 2)).astype(f32)
    base = ((half + f32(0.4 * HD)) / f32(1.4 * HD)).astype(f32)
    power = ((pos - SEQ // 2) / (WINDOW // 2)).astype(f32)
    scale = np.tile(np.power(base[None, :], power[:, None]), (1, 2)).astype(f32)
    cos, sin = np.cos(freqs), np.sin(freqs)
    sin[:, :HD // 2] *= -1
    rot = np.stack([np.stack([cos * scale, sin * scale], 1), np.stack([cos / scale, sin / scale], 1)], 1)
    c["c_rot"] = np.ascontiguousarray(np.tile(rot, (2, 1, 1, 1)), dtype=f32)
    c["c_heads8"] = (t[:, None] // SD == np.arange(HEADS)[None, :]).astype(f32)
    return c


def kernel(**inputs):
    import concourse.bacc as bacc
    from concourse.bass_utils import run_bass_kernel_spmd as run

    a = {k: np.asarray(v) for k, v in inputs.items()}
    arrays = dict(
        x=a["x"], ctx_in=a["ctx_1024"], mask=a["mask_BxS2_bk0"].reshape(1, -1).view(np.int32),
        params=a["L0_attn_params"], wvT=a["L0_attn_Wv"].T, bv=a["L0_attn_bv"].reshape(1, -1),
        woT_a=a["L0_attn_Wo"].T, bo=a["L0_attn_bo"].reshape(1, -1),
        wq=a["L0_xattn_W_Q"], wk=a["L0_xattn_W_K"], wv=a["L0_xattn_W_V"], wo_x=a["L0_xattn_W_O"],
        wqkv=a["L0_ffn_Wqkv"], q_scale=a["L0_ffn_q_scale"], k_scale=a["L0_ffn_k_scale"], wo=a["L0_ffn_Wo"],
        ln_gT=a["L0_ffn_ln_g"].T, ln_bT=a["L0_ffn_ln_b"].T, w1=a["L0_ffn_W1"], b1T=a["L0_ffn_b1"].T,
        w2=a["L0_ffn_W2"], b2=a["L0_ffn_b2"], **constants())
    nc = bacc.Bacc("TRN2", target_bir_lowering=False, num_devices=1)
    feeds, aps = {}, []
    for name, v in arrays.items():
        v = np.ascontiguousarray(v)
        feeds["in_" + name] = v
        aps.append(nc.dram_tensor("in_" + name, v.shape, mybir.dt.from_np(v.dtype), kind="ExternalInput").ap())
    aps.append(nc.dram_tensor("out_0", (BATCH, SEQ, DIM), FP32, kind="ExternalOutput").ap())
    build(nc, *aps)
    r = run(nc, [feeds], core_ids=[0])
    return r.results[0]["out_0"]
```

```python
import numpy as np
from contextlib import ExitStack

import concourse.bass as bass
from concourse import mybir

FP32, BF16, I32, U8 = mybir.dt.float32, mybir.dt.bfloat16, mybir.dt.int32, mybir.dt.uint8
ALU = mybir.AluOpType
ACT = mybir.ActivationFunctionType
AX = mybir.AxisListType

BATCH, SEQ, DIM = 64, 64, 128
TILES = BATCH * SEQ // 128
HEADS, PAIRS = 16, 8
HD = 64
SD = DIM // HEADS
DEPTH, WINDOW = 6, 32
INNER = HEADS * HD
FF = int(DIM * 4 * 2 / 3)
FF_CHUNKS = [(c * 128, min(128, FF - c * 128)) for c in range(3)]
FF_BANKS = (6, 7, 5)
MASKED = -1.0e37
RSQRT_MAGIC = float(0x5F3759DF)
EPS = 1e-5


class Names:
    pass


def at_least(eng, sem, value):
    if not isinstance(value, int) or value > 0:
        eng.wait_ge(sem, value)


def hold(eng, held):
    eng.sem_inc(held, 1)


def run_pipeline(eng, turn, tiles):
    turn(-1, 1, True, False, False, False)
    turn(0, 0, True, True, False, False)
    turn(1, 1, True, True, True, False)
    turn(2, 0, True, True, True, True)
    turn(3, 1, True, True, True, True)
    with eng.Fori(4, tiles - 3, 2) as i:
        turn(i, 0, True, True, True, True)
        turn(i + 1, 1, True, True, True, True)
    turn(tiles - 2, 0, True, True, True, True)
    turn(tiles - 1, 1, False, True, True, True)
    turn(tiles, 0, False, False, True, True)
    turn(tiles + 1, 1, False, False, False, True)
    turn(tiles + 2, 0, False, False, False, False)


def trails(i, par, pair=False):
    return (par == 0 or not pair) and (not isinstance(i, int) or i >= (4 if pair else 3))


def capped(i, n):
    return min(i, n) if isinstance(i, int) else i


def within(i, low, high):
    return not isinstance(i, int) or low <= i <= high


def flat(ap):
    return ap.rearrange("p a b -> p (a b)")


def build(nc, x, ctx_in, mask, params, wvT, bv, woT_a, bo, wq, wk, wv, wo_x, wqkv, q_scale, k_scale, wo,
          ln_gT, ln_bT, w1, b1T, w2, b2, c_ident, c_shift, c_causal, c_rot, c_heads8, out):
    es = ExitStack()
    with es:
        def sb(name, shape, dt=FP32):
            return es.enter_context(nc.sbuf_tensor(name, shape, dt))

        def sem(name):
            return es.enter_context(nc.semaphore(name))

        m = Names()
        m.x, m.ctx_in, m.mask, m.params, m.wvT, m.bv = x, ctx_in, mask, params, wvT, bv
        m.woT_a, m.bo, m.wq, m.wk, m.wv, m.wo_x = woT_a, bo, wq, wk, wv, wo_x
        m.wqkv, m.q_scale, m.k_scale, m.wo, m.ln_gT, m.ln_bT = wqkv, q_scale, k_scale, wo, ln_gT, ln_bT
        m.w1, m.b1T, m.w2, m.b2, m.c_ident, m.c_shift = w1, b1T, w2, b2, c_ident, c_shift
        m.c_causal, m.c_rot, m.c_heads8, m.out = c_causal, c_rot, c_heads8, out

        m.X = sb("X", [128, TILES, DIM])
        m.Y = sb("Y", [128, TILES, DIM])
        m.WA = sb("WA", [128, 3 * INNER])
        m.WO = sb("WO", [128, PAIRS * DIM])
        m.W1 = sb("W1", [128, 2 * FF])
        m.W2 = sb("W2", [128, 3 * DIM])
        m.ident = sb("ident", [128, 128])
        m.identb = sb("identb", [128, 128], BF16)
        m.shift = sb("shift", [128, 128])
        m.causal = sb("causal", [128, 512])
        m.causalb = sb("causalb", [128, 512], BF16)
        m.rot = sb("rot", [128, 2, 2, HD])
        m.scales = sb("scales", [128, 2, 2, DEPTH, HD])
        m.tables = sb("tables", [128, DEPTH, 2, 2, HD])
        m.heads8 = sb("heads8", [128, HEADS])
        m.gcol = sb("gcol", [128, DEPTH])
        m.bcol = sb("bcol", [128, DEPTH])
        m.b1col = sb("b1col", [128, 2, 3, DEPTH])
        m.ones = sb("ones", [1, 128])
        m.onesb = sb("onesb", [1, 128], BF16)
        m.minus_half = sb("minus_half", [128, 1])
        m.bvrow = sb("bvrow", [1, DIM])
        m.borow = sb("borow", [1, DIM])
        m.tril = sb("tril", [128, SD])
        m.trilbd = sb("trilbd", [128, 128])
        m.trilT = sb("trilT", [128, 128])
        m.wqk = sb("wqk", [128, 128])
        m.wvT_sb = sb("wvT_sb", [128, 128])
        m.woT_sb = sb("woT_sb", [128, 128])
        m.mask8 = sb("mask8", [1, BATCH * SEQ // 4], I32)
        m.maskb = sb("maskb", [1, BATCH * SEQ], BF16)
        m.maskrow = sb("maskrow", [1, 2, 4, 128], BF16)
        m.ctx_sb = sb("ctx_sb", [128, 2, DIM])
        m.ystat = sb("ystat", [128, DIM])
        m.xsT = sb("xsT", [128, 2, 2, SEQ])
        m.xsT_shifted = sb("xsT_shifted", [128, 2, 2, SEQ])
        m.ctxT = sb("ctxT", [128, 2, 128])
        m.sq = sb("sq", [128, 2048])
        m.ss = sb("ss", [128, 32])
        m.ssm = sb("ssm", [128, 32])
        m.bits = sb("bits", [128, 32], I32)
        m.seed = sb("seed", [128, 32], I32)
        m.rn = sb("rn", [128, 32])
        m.rn_a = sb("rn_a", [128, 32])
        m.rn_b = sb("rn_b", [128, 32])
        m.qn = sb("qn", [128, 2048])
        m.RA = sb("RA", [128, 2048])
        m.RB = sb("RB", [128, 2048])
        m.qTbd = sb("qTbd", [128, PAIRS, 2, 2, SEQ])
        m.kT = sb("kT", [128, PAIRS * 128])
        m.V = sb("V", [128, 2, HEADS * HD])
        m.D = sb("D", [128, 1024])
        m.P = sb("P", [128, 1024])
        m.mx = sb("mx", [128, 16])
        m.PTbd = sb("PTbd", [128, HEADS, 2, SEQ])
        m.row_sum = sb("row_sum", [128, 16])
        m.inv_sum = sb("inv_sum", [128, 16])
        m.OT = sb("OT", [128, PAIRS * 128])
        m.y1 = sb("y1", [128, 2, DIM])
        m.ys = sb("ys", [128, DIM])
        m.stats = sb("stats", [128, 6])
        m.mv = sb("mv", [128, 2])
        m.vare = sb("vare", [128, 1])
        m.rstd = sb("rstd", [128, 1])
        m.xn = sb("xn", [128, DIM])
        m.xnT = sb("xnT", [128, 2, 128])
        m.G = sb("G", [128, 3, 256])
        m.H = sb("H", [128, 3, 256])
        m.bank = [es.enter_context(nc.psum_tensor(f"bank{n}", [128, 512], FP32)) for n in range(8)]

        m.cross_w = sem("cross_weights")

        setup(nc, sem, m)
        for kind in ("self", "cross", "local"):
            stage(nc, sem, kind, m)
        finish(nc, sem, m)


def setup(nc, sem, m):
    dma, dmac = sem("setup_dma"), sem("setup_tril_zero")
    cast, zeroed, made = sem("setup_cast"), sem("setup_zeroed"), sem("setup_made")
    tril_done, tril_copied, norm = sem("setup_tril_done"), sem("setup_tril_copied"), sem("setup_norm")
    held = sem("setup_held")
    var, rstd_done, small = sem("setup_var"), sem("setup_rstd"), sem("setup_small")
    loads = [
        (m.X[:, :, :], m.x.rearrange("(t b) s d -> (b s) t d", b=2)),
        (m.ident[:, :], m.c_ident), (m.shift[:, :], m.c_shift), (m.causal[:, :], m.c_causal),
        (m.rot[:, :, :, :], m.c_rot), (m.heads8[:, :], m.c_heads8),
        (m.gcol[:, :], m.ln_gT), (m.bcol[:, :], m.ln_bT), (m.bvrow[:, :], m.bv), (m.borow[:, :], m.bo),
        (m.wvT_sb[:, :], m.wvT), (m.woT_sb[:, :], m.woT_a), (m.mask8[:, :], m.mask),
    ]
    for side in range(2):
        for c, (at, rows) in enumerate(FF_CHUNKS):
            loads.append((m.b1col[0:rows, side, c, :], m.b1T[side * FF + at:side * FF + at + rows, :]))
    half = HD // 2
    for n, s in enumerate((m.q_scale, m.k_scale)):
        wide = s.rearrange("l (a d) -> a l d", a=1)
        loads.append((m.scales[:, n, 0, :, :], wide.to_broadcast([128, DEPTH, HD])))
        for to, frm in ((0, half), (half, 0)):
            loads.append((m.scales[:, n, 1, :, to:to + half],
                          wide[:, :, frm:frm + half].to_broadcast([128, DEPTH, half])))
    with nc.Block() as block:

        @block.sync
        def _(sp):
            for dst, src in loads:
                sp.dma_start(dst, src).then_inc(dma, 16)
            sp.wait_ge(dmac, 1)
            for i in range(SD):
                off = i * (i + 1) // 2
                sp.dma_start(m.tril[i:128:SD, 0:i + 1], m.params[:, off:off + i + 1],
                             allow_slow_non_contiguous=True).then_inc(tril_done, 16)

        @block.gpsimd
        def _(pool):
            pool.memset(m.tril[:, :], 0.0).then_inc(dmac, 1)
            pool.memset(m.ones[:, :], 1.0)
            pool.memset(m.onesb[:, :], 1.0)
            pool.memset(m.minus_half[:, :], -0.5).then_inc(zeroed, 1)
            pool.memset(m.qTbd[:, :, :, :, :], 0.0)
            pool.memset(m.PTbd[:, :, :, :], 0.0)
            pool.memset(m.H[:, :, :], 1.0)
            pool.memset(m.qn[:, :], 0.0)
            pool.memset(m.RB[:, :], 0.0)
            pool.memset(m.xsT_shifted[:, :, :, :], 0.0)

            def inverse_root(t):
                at_least(pool, rstd_done, t)
                pool.wait_ge(var, t + 1)
                hold(pool, held)
                pool.tensor_scalar(m.vare[:, :], m.mv[:, 1:2], EPS, None, ALU.add).then_inc(small, 1)
                pool.wait_ge(small, t + 1)
                pool.tensor_tensor(m.rstd[:, :], m.vare[:, :], m.minus_half[:, :], ALU.pow).then_inc(rstd_done, 1)

            inverse_root(0)
            with pool.Fori(1, TILES, 1) as t:
                inverse_root(t)

        @block.vector
        def _(dve):
            dve.wait_ge(dma, 16 * len(loads))
            dve.tensor_copy(m.identb[:, :], m.ident[:, :]).then_inc(cast, 1)
            dve.tensor_copy(m.causalb[:, :], m.causal[:, :]).then_inc(cast, 1)
            dve.tensor_scalar(m.maskb[:, :], m.mask8[:, :].bitcast(U8), MASKED, None, ALU.mult).then_inc(cast, 1)
            for n in range(2):
                for s in range(2):
                    dve.tensor_tensor(m.tables[:, :, n, s, :], m.scales[:, n, s, :, :],
                                      m.rot[:, n, s, :].unsqueeze(1).to_broadcast([128, DEPTH, HD]), ALU.mult)
            dve.wait_ge(tril_done, 16 * SD)
            dve.tensor_tensor(m.trilbd[:, :].rearrange("p (h j) -> p h j", j=SD),
                              m.tril[:, :].unsqueeze(1).to_broadcast([128, HEADS, SD]),
                              m.heads8[:, :].unsqueeze(2).to_broadcast([128, HEADS, SD]), ALU.mult).then_inc(made, 1)

            def normalise(t):
                at_least(dve, norm, t)
                hold(dve, held)
                dve.bn_stats(m.stats[:, :], m.X[:, bass.ds(t, 1), :]).then_inc(cast, 1)
                dve.wait_ge(cast, t + 4)
                hold(dve, held)
                dve.bn_aggr(m.mv[:, :], m.stats[:, :]).then_inc(var, 1)
                dve.wait_ge(rstd_done, t + 1)
                dve.tensor_scalar(m.Y[:, bass.ds(t, 1), :], m.X[:, bass.ds(t, 1), :], m.mv[:, 0:1], m.rstd[:, 0:1],
                                  ALU.subtract, ALU.mult).then_inc(norm, 1)

            normalise(0)
            with dve.Fori(1, TILES, 1) as t:
                normalise(t)

        @block.tensor
        def _(pe):
            pe.wait_ge(made, 1)
            pe.transpose(m.bank[0][:, 0:128], m.trilbd[:, :], m.ident[:, :]).then_inc(tril_copied, 1)
            pe.wait_ge(made, 2)
            pe.matmul(m.bank[1][:, 0:128], m.trilT[:, :], m.trilT[:, :], start=True, stop=True).then_inc(tril_copied, 1)

        @block.scalar
        def _(act):
            act.wait_ge(tril_copied, 1)
            act.activation(m.trilT[:, :], m.bank[0][:, 0:128], ACT.Copy).then_inc(made, 1)
            act.wait_ge(tril_copied, 2)
            act.activation(m.wqk[:, :], m.bank[1][:, 0:128], ACT.Copy).then_inc(made, 1)


def finish(nc, sem, m):
    summed, stored = sem("finish_summed"), sem("finish_stored")
    parts = 4
    n = TILES // parts
    out = m.out.rearrange("(t b) s d -> (b s) t d", b=2)
    with nc.Block() as block:

        @block.vector
        def _(dve):
            for c in range(parts):
                part = slice(c * n, (c + 1) * n)
                dve.tensor_tensor(m.X[:, part, :], m.X[:, part, :], m.Y[:, part, :], ALU.add).then_inc(summed, 1)

        @block.sync
        def _(sp):
            for c in range(parts):
                part = slice(c * n, (c + 1) * n)
                sp.wait_ge(summed, c + 1)
                sp.dma_start(out[:, part, :], m.X[:, part, :]).then_inc(stored, 16)
            sp.wait_ge(stored, 16 * parts)


def stage(nc, sem, kind, m):
    SELF, CROSS, LOCAL = kind == "self", kind == "cross", kind == "local"
    N = TILES * DEPTH if LOCAL else TILES
    EXP_SCALE = {"self": SD ** -0.5, "cross": HD ** -0.5, "local": 8.0}[kind]
    NPRE = 1 if SELF else 2
    NQT, NKT = (2, 1) if SELF else (4, 2)
    NV = NO = 1 if SELF else 2
    NRN = 12
    b = m.bank
    s = Names()
    s.w_in = sem(f"{kind}_w_in")
    s.w_out = sem(f"{kind}_w_out")
    s.ystat = sem(f"{kind}_ystat")
    s.pre_t = sem(f"{kind}_pre_t")
    s.pre_copied = sem(f"{kind}_pre_copied")
    s.qk = sem(f"{kind}_qk")
    s.qT = sem(f"{kind}_qT")
    s.kT = sem(f"{kind}_kT")
    s.v = sem(f"{kind}_v")
    s.v_copied = sem(f"{kind}_v_copied")
    s.scores = sem(f"{kind}_scores")
    s.mx = sem(f"{kind}_mx")
    s.diff = sem(f"{kind}_diff")
    s.probs = sem(f"{kind}_probs")
    s.pt = sem(f"{kind}_pt")
    s.pt_copied = sem(f"{kind}_pt_copied")
    s.o = sem(f"{kind}_o")
    s.row_sum = sem(f"{kind}_row_sum")
    s.pnorm = sem(f"{kind}_pnorm")
    s.recip = sem(f"{kind}_recip")
    s.ot_copied = sem(f"{kind}_ot_copied")
    s.wo = sem(f"{kind}_wo")
    s.y1 = sem(f"{kind}_y1")
    s.stats = sem(f"{kind}_stats")
    s.var = sem(f"{kind}_var")
    s.vare = sem(f"{kind}_vare")
    s.rstd = sem(f"{kind}_rstd")
    s.xn = sem(f"{kind}_xn")
    if CROSS:
        s.ctx_even = sem(f"{kind}_ctx_even")
        s.ctx_odd = sem(f"{kind}_ctx_odd")
        s.mask_made = sem(f"{kind}_mask_made")
    if LOCAL:
        s.w_values = sem(f"{kind}_w_values")
        s.w_ff = sem(f"{kind}_w_ff")
        s.sq = sem(f"{kind}_sq")
        s.ss = sem(f"{kind}_ss")
        s.seed = sem(f"{kind}_seed")
        s.newton = sem(f"{kind}_newton")
        s.qn = sem(f"{kind}_qn")
        s.ra = sem(f"{kind}_ra")
        s.half = sem(f"{kind}_half")
        s.rotated = sem(f"{kind}_rotated")
        s.rot = sem(f"{kind}_rot")
        s.sh = sem(f"{kind}_sh")
        s.sh_copied = sem(f"{kind}_sh_copied")
        s.ys = sem(f"{kind}_ys")
        s.xn_t = sem(f"{kind}_xn_t")
        s.xn_copied = sem(f"{kind}_xn_copied")
        s.ff = sem(f"{kind}_ff")
        s.gelu = sem(f"{kind}_gelu")
        s.h = sem(f"{kind}_h")
        s.w2 = sem(f"{kind}_w2")
        s.y = sem(f"{kind}_y")
    held = sem(f"{kind}_held")
    V = [m.qn[:, :], m.RB[:, :]] if SELF else [m.V[:, 0, :], m.V[:, 1, :]]
    qTbd = m.RA[:, :].rearrange("p (h t a q) -> p h t a q", h=PAIRS, t=2, a=2) if SELF else m.qTbd
    xsT_tokens = m.xsT_shifted if LOCAL else m.xsT
    xsT = [flat(xsT_tokens[:, n, :, :]) for n in range(2)]

    def slot(t):
        return t % TILES if LOCAL else t

    def tile_of(buf, t):
        return flat(buf[:, bass.ds(slot(t), 1), :])

    with nc.Block() as block:

        @block.sync
        def _(sp):
            if SELF:
                for c, w in enumerate((m.wq, m.wk, m.wv)):
                    sp.dma_start(m.WA[:, c * INNER:(c + 1) * INNER], w).then_inc(m.cross_w, 16)
                sp.dma_start(m.WO[:, :].rearrange("p (c n) -> p c n", n=DIM),
                             m.wo_x.rearrange("(c p) n -> p c n", p=128)).then_inc(m.cross_w, 16)
            if CROSS:
                ctx_tiles = m.ctx_in.rearrange("(t b) s d -> t (b s) d", b=2)

                def load_ctx(t, par):
                    at_least(sp, s.pre_t, t - 1)
                    sp.dma_start(m.ctx_sb[:, par, :], flat(ctx_tiles[bass.ds(t, 1), :, :].rearrange("a p d -> p a d")))\
                      .then_inc((s.ctx_even, s.ctx_odd)[par], 16)

                load_ctx(0, 0)
                load_ctx(1, 1)
                with sp.Fori(2, N - 1, 2) as t:
                    load_ctx(t, 0)
                    load_ctx(t + 1, 1)
            if LOCAL:
                def load_in(l):
                    sp.dma_start(m.WA[:, 0:2 * INNER], flat(m.wqkv[bass.ds(l, 1), :, 0:2 * INNER].rearrange("a p n -> p a n")))\
                      .then_inc(s.w_in, 16)

                def load_values(l):
                    sp.dma_start(m.WA[:, 2 * INNER:], flat(m.wqkv[bass.ds(l, 1), :, 2 * INNER:].rearrange("a p n -> p a n")))\
                      .then_inc(s.w_values, 16)

                def load_out(l):
                    sp.dma_start(m.WO[:, :].rearrange("p (c n) -> p c n", n=DIM),
                                 m.wo[bass.ds(l, 1), :, :].rearrange("a (c p) n -> p (a c) n", p=128)).then_inc(s.w_out, 16)

                def load_ff(l):
                    at, rows = FF_CHUNKS[2]
                    one = bass.ds(l, 1)
                    sp.dma_start(m.W1[:, :], flat(m.w1[one, :, :].rearrange("a p n -> p a n"))).then_inc(s.w_ff, 16)
                    sp.dma_start(m.W2[:, 0:2 * DIM].rearrange("p (c n) -> p c n", n=DIM),
                                 m.w2[one, 0:at, :].rearrange("a (c p) n -> p (a c) n", p=128)).then_inc(s.w_ff, 16)
                    sp.dma_start(m.W2[0:rows, 2 * DIM:3 * DIM],
                                 flat(m.w2[one, at:FF, :].rearrange("a p n -> p a n"))).then_inc(s.w_ff, 16)
                    sp.dma_start(m.W2[rows:rows + 1, 2 * DIM:3 * DIM], m.b2[one, :]).then_inc(s.w_ff, 16)

                load_in(0)
                load_values(0)
                load_out(0)
                load_ff(0)
                with sp.Fori(1, DEPTH, 1) as l:
                    sp.wait_ge(s.qk, 4 * TILES * l)
                    load_in(l)
                    sp.wait_ge(s.v, NV * TILES * l)
                    load_values(l)
                    sp.wait_ge(s.wo, TILES * l)
                    load_out(l)
                    sp.wait_ge(s.w2, TILES // 2 * l)
                    load_ff(l)

        @block.tensor
        def _(pe):
            mm = nc.tensor.matmul

            def out_projection(t):
                pe.wait_ge(s.ot_copied, NO * (t + 1))
                if SELF:
                    mm(b[4][:, 0:128], m.OT[:, 0:128], m.woT_sb[:, :], start=True, stop=False)
                    mm(b[4][:, 0:128], m.ones[:, :], m.borow[:, :], start=False, stop=True).then_inc(s.wo, 1)
                    return
                if LOCAL:
                    pe.wait_ge(s.w_out, 16 * (t // TILES) + 16)
                for c in range(PAIRS):
                    last = mm(b[4][:, 0:128], m.OT[:, c * 128:(c + 1) * 128], m.WO[:, c * 128:(c + 1) * 128],
                              start=(c == 0), stop=(c == PAIRS - 1))
                last.then_inc(s.wo, 1)

            def bank_copied(t, c):
                if c < 2:
                    at_least(pe, s.qT, NQT * (t - 1) + 2 * c + 2)
                else:
                    at_least(pe, s.kT, NKT * (t - 1) + c - 1)

            def input_transposed(i):
                pe.wait_ge(s.xn, i - 2)
                pe.wait_ge(s.v_copied, NV * capped(i, N) - 1)
                nc.tensor.transpose(b[6][:, 0:128], m.xn[:, :], m.ident[:, :]).then_inc(s.xn_t, 1)

            def queries_keys(t, par, between):
                pe.wait_ge(s.pre_copied, NPRE * (t + 1))
                if SELF:
                    at_least(pe, s.qT, NQT * t)
                    mm(b[0][:, 0:128], m.wqk[:, :], xsT[par], start=True, stop=True).then_inc(s.qk, 1)
                if CROSS:
                    if isinstance(t, int) and t == 0:
                        pe.wait_ge(m.cross_w, 64)
                    for c in range(4):
                        bank_copied(t, c)
                        for n in range(4):
                            at = c * 512 + n * 128
                            last = mm(b[c][:, n * 128:(n + 1) * 128], m.WA[:, at:at + 128],
                                      xsT[par] if c < 2 else m.ctxT[:, par, :], start=True, stop=True)
                        last.then_inc(s.qk, 1)
                if LOCAL:
                    pe.wait_ge(s.w_in, 16 * (t // TILES) + 16)
                    for c in range(4):
                        between(c)
                        bank_copied(t, c)
                        mm(b[c][:, :], xsT[par], m.WA[:, c * 512:(c + 1) * 512], start=True, stop=True).then_inc(s.qk, 1)

            def values(t, par, c):
                at_least(pe, s.v_copied, NV * t)
                if SELF:
                    mm(b[6][:, 0:128], xsT[par], m.wvT_sb[:, :], start=True, stop=False)
                    mm(b[6][:, 0:128], m.ones[:, :], m.bvrow[:, :], start=False, stop=True).then_inc(s.v, 1)
                    return
                if LOCAL:
                    pe.wait_ge(s.w_values, 16 * (t // TILES) + 16)
                at = 2 * INNER + c * 512
                mm(b[6 + c][:, :], xsT[par] if LOCAL else m.ctxT[:, par, :], m.WA[:, at:at + 512],
                   start=True, stop=True).then_inc(s.v, 1)

            def scores(t, par, late):
                pe.wait_ge(s.qT, NQT * (t + 1))
                pe.wait_ge(s.kT, NKT * (t + 1))
                at_least(pe, s.pt_copied, 4 * t)
                if CROSS:
                    pe.wait_ge(s.mask_made, t + 1)
                for j in range(2):
                    if j == 1 and late:
                        pe.wait_ge(s.h, 3 * ((t - 3) // 2) + 3)
                    if CROSS:
                        mm(b[4 + j][:, :], m.onesb[:, :], m.maskrow[:, par, :, :].rearrange("p a k -> p (a k)"),
                           start=True, stop=False)
                    if LOCAL:
                        mm(b[4 + j][:, :], m.identb[:, :], m.causalb[:, :], start=True, stop=False)
                    for n in range(8):
                        hp, bb = 4 * j + n // 2, n % 2
                        keys = bb * 64 if SELF else hp * 128 + bb * 64
                        last = mm(b[4 + j][:, n * 64:(n + 1) * 64], flat(qTbd[:, hp, bb, :, :]),
                                  m.kT[:, keys:keys + 64], start=SELF, stop=SELF or n == 7)
                    last.then_inc(s.scores, 1)

            def probs_transposed(t, j):
                pe.wait_ge(s.pnorm, 2 * t + j + 1)
                for n in range(4):
                    c = 4 * j + n
                    last = nc.tensor.transpose(b[4 + j][:, n * 128:(n + 1) * 128], m.P[:, c * 128:(c + 1) * 128],
                                               m.ident[:, :])
                last.then_inc(s.pt, 1)

            def rotated_transposed(t, j):
                pe.wait_ge(s.qn, 4 * t + j + 1)
                for n in range(4):
                    at, col = j * 512 + n * 128, n * 128
                    last = nc.tensor.transpose(b[j][:, col:col + 128], m.qn[:, at:at + 128], m.ident[:, :])
                last.then_inc(s.rot, 1)

            def head_outputs(i, par):
                t = i - 2
                outputs_bank_free(i, par, 0)
                pe.wait_ge(s.v_copied, NV * (t + 1))
                pe.wait_ge(s.pt_copied, 4 * (t + 1))
                for h in range(HEADS):
                    if h == 8 and NO == 2:
                        outputs_bank_free(i, par, 1)
                    probs = flat(m.PTbd[:, h, :, :])
                    if SELF:
                        last = mm(b[6][:, 0:128], V[par][:, h * DIM:(h + 1) * DIM], probs,
                                  start=(h == 0), stop=(h == HEADS - 1))
                        continue
                    rows, col = slice(HD * (h % 2), HD * (h % 2) + HD), h // 2 % 4 * 128
                    last = mm(b[6 + h // 8][rows, col:col + 128], V[par][:, h * HD:(h + 1) * HD], probs,
                              start=True, stop=True)
                    if h == 7:
                        last.then_inc(s.o, 1)
                last.then_inc(s.o, 1)

            def pre_transposed(t, par):
                pe.wait_ge(s.ystat, t + 1)
                last = nc.tensor.transpose(b[5][:, 0:128], m.ystat[:, :], m.ident[:, :])
                if CROSS:
                    pe.wait_ge((s.ctx_even, s.ctx_odd)[par], 16 * ((t - par) // 2) + 16)
                    last = nc.tensor.transpose(b[5][:, 128:256], m.ctx_sb[:, par, :], m.ident[:, :])
                last.then_inc(s.pre_t, 1)

            def feed_forward_in(t, c):
                pe.wait_ge(s.w_ff, 64 * (t // TILES) + 64)
                at, rows = FF_CHUNKS[c]
                bk = b[FF_BANKS[c]]
                for side, off in ((0, FF), (1, 0)):
                    last = mm(bk[0:rows, side * 256:(side + 1) * 256], m.W1[:, off + at:off + at + rows],
                              flat(m.xnT[:, :, :]), start=True, stop=True)
                last.then_inc(s.ff, 1)

            def feed_forward_out(t):
                pe.wait_ge(s.h, 3 * ((t - 1) // 2) + 3)
                for n in range(2):
                    for c, (_, rows) in enumerate(FF_CHUNKS):
                        k = rows + (c == 2)
                        last = mm(b[7][:, n * 128:(n + 1) * 128], m.H[0:k, c, n * 128:(n + 1) * 128],
                                  m.W2[0:k, c * 128:(c + 1) * 128], start=(c == 0), stop=(c == 2))
                last.then_inc(s.w2, 1)

            def outputs_bank_free(i, par, j):
                static = isinstance(i, int)
                pe.wait_ge(s.v_copied, NV * (min(i, N) if static else i))
                if LOCAL:
                    at_least(pe, s.xn_copied, i - 2)
                    if trails(i, par, pair=True):
                        if j == 0:
                            pe.wait_ge(s.h, 3 * ((i - 4) // 2) + 1)
                        else:
                            pe.wait_ge(s.y, TILES // 2 + (i - 2) // 2)

            def turn(i, par, pre, head, mid, tail):
                late = LOCAL and trails(i, par, pair=True)

                def between(c):
                    if c == 2:
                        if within(i, 1, N):
                            rotated_transposed(i - 1, 3)
                    if c == 4:
                        if within(i, 2, N + 1):
                            at_least(pe, s.sh_copied, i - 2)
                            probs_transposed(i - 2, 0)
                        if within(i, 2, N + 1):
                            pe.wait_ge(s.pre_copied, NPRE * capped(i + 1, N))
                            probs_transposed(i - 2, 1)
                        if trails(i, par):
                            input_transposed(i)
                        if within(i, 1, N):
                            values(i - 1, 1 - par, 1)

                if head:
                    queries_keys(i, par, between)
                elif LOCAL:
                    between(2)
                if LOCAL:
                    between(4)
                if late:
                    pe.wait_ge(s.xn_copied, i - 2)
                    for c in range(3):
                        if c == 1:
                            pe.wait_ge(s.v_copied, NV * capped(i, N))
                        if c == 2:
                            static = isinstance(i, int)
                            pe.wait_ge(s.pt_copied, 4 * (min(i - 1, N) if static else i - 1))
                        feed_forward_in(i - 3, c)
                if mid:
                    scores(i - 1, 1 - par, late)
                if tail and not late:
                    head_outputs(i, par)
                if late:
                    feed_forward_out(i - 3)
                    if tail:
                        head_outputs(i, par)
                if head and LOCAL:
                    rotated_transposed(i, 0)
                if pre and not LOCAL:
                    if mid:
                        pe.wait_ge(s.diff, 2 * i)
                    pre_transposed(i + 1, 1 - par)
                if tail:
                    if mid:
                        pe.wait_ge(s.diff, 2 * (i - 1) + 1)
                    out_projection(i - 2)
                if pre and LOCAL:
                    if mid:
                        pe.wait_ge(s.diff, 2 * i)
                    pre_transposed(i + 1, 1 - par)
                if head and not late:
                    values(i, par, 0)
                if head and LOCAL:
                    for j in range(1, 3):
                        rotated_transposed(i, j)
                if tail and LOCAL:
                    pe.wait_ge(s.y1, i - 1)
                    pe.wait_ge(s.ys, i - 1)
                    mm(b[4][:, 128:192], m.shift[:, :], m.y1[:, par, 64:128], start=True, stop=True).then_inc(s.sh, 1)
                if head and late:
                    values(i, par, 0)
                if head and CROSS:
                    values(i, par, 1)
                if mid and not LOCAL:
                    if tail:
                        pe.wait_ge(s.y1, i - 1)
                    probs_transposed(i - 1, 0)
                    if pre:
                        pe.wait_ge(s.pre_copied, NPRE * (i + 2))
                    probs_transposed(i - 1, 1)

            run_pipeline(pe, turn, N)

        @block.scalar
        def _(act):
            def copy(dst, src):
                return nc.scalar.activation(dst, src, ACT.Copy)

            def values_out(i, par, j):
                act.wait_ge(s.v, NV * i + j + 1)
                if SELF:
                    blocks = V[par][:, 0:HEADS * DIM].rearrange("p (h g d) -> p h g d", h=HEADS, d=SD)
                    for h in range(HEADS):
                        last = copy(blocks[:, h, h, :], b[6][:, h * SD:(h + 1) * SD])
                    last.then_inc(s.v_copied, 1)
                else:
                    copy(V[par][:, j * 512:(j + 1) * 512], b[6 + j][:, :]).then_inc(s.v_copied, 1)

            def probs_out(t, j):
                act.wait_ge(s.pt, 2 * t + j + 1)
                for bb in range(2):
                    rows = slice(64 * bb, 64 * bb + 64)
                    copy(m.PTbd[rows, 8 * j:8 * j + 8, bb, :],
                         b[4 + j][rows, :].rearrange("p (h q) -> p h q", q=SEQ)).then_inc(s.pt_copied, 1)

            def input_out(i, par):
                act.wait_ge(s.xn_t, i - 2)
                l = (i - 3) // TILES
                nc.scalar.activation(m.xnT[:, 1 - par, :], b[6][:, 0:128], ACT.Identity, scale=m.gcol[:, bass.ds(l, 1)],
                                     bias=m.bcol[:, bass.ds(l, 1)]).then_inc(s.xn_copied, 1)

            def gates(t, c):
                act.wait_ge(s.ff, 3 * ((t - 1) // 2) + c + 1)
                rows = FF_CHUNKS[c][1]
                nc.scalar.activation(m.G[0:rows, c, :], b[FF_BANKS[c]][0:rows, 0:256], ACT.Gelu,
                                     bias=m.b1col[0:rows, 1, c, bass.ds(t // TILES, 1)]).then_inc(s.gelu, 1)

            def queries_out(i, ready, j):
                at_least(act, s.scores, 2 * i)
                act.wait_ge(ready, 4 * i + j + 1)
                for a in range(2):
                    rows = slice(64 * a, 64 * a + 64)
                    copy(qTbd[rows, 4 * j:4 * j + 4, :, a, :],
                         b[j][rows, :].rearrange("p (h t q) -> p h t q", h=4, q=SEQ)).then_inc(s.qT, 1)

            def outputs_out(i):
                for j in range(NO):
                    act.wait_ge(s.o, NO * (i - 2) + j + 1)
                    n = 128 if SELF else 512
                    copy(m.OT[:, j * n:(j + 1) * n], b[6 + j][:, 0:n]).then_inc(s.ot_copied, 1)

            def keys_out(i, ready, j):
                act.wait_ge(ready, 4 * i + 2 + j + 1)
                copy(m.kT[:, j * 512:(j + 1) * 512], b[2 + j][:, :]).then_inc(s.kT, 1)

            def turn(i, par, pre, head, mid, tail):
                late = LOCAL and trails(i, par, pair=True)
                ready = s.rot if LOCAL else s.qk
                if LOCAL:
                    for j in range(4):
                        if j == 2 and within(i, 1, N):
                            keys_out(i - 1, ready, 1)
                        if head:
                            act.wait_ge(s.qk, 4 * i + j + 1)
                            at_least(act, s.ss, 4 * (i - 1) + j + 1)
                            nc.scalar.activation(m.sq[:, j * 512:(j + 1) * 512], b[j][:, :], ACT.Square).then_inc(s.sq, 1)
                    if within(i, 2, N + 1):
                        probs_out(i - 2, 0)
                        probs_out(i - 2, 1)
                    if trails(i, par):
                        input_out(i, par)
                    if within(i, 1, N):
                        values_out(i - 1, 1 - par, 1)
                if late:
                    at_least(act, s.h, 3 * ((i - 4) // 2))
                    for c in range(3):
                        gates(i - 3, c)
                if mid:
                    for j in range(2):
                        act.wait_ge(s.diff, 2 * (i - 1) + j + 1)
                        nc.scalar.activation(m.P[:, j * 512:(j + 1) * 512], m.D[:, j * 512:(j + 1) * 512], ACT.Exp,
                                             scale=EXP_SCALE).then_inc(s.probs, 1)
                if head and SELF:
                    at_least(act, s.scores, 2 * i)
                    act.wait_ge(s.pre_copied, i + 1)
                    copy(m.kT[:, 0:128], xsT[par]).then_inc(s.kT, 1)
                if tail:
                    outputs_out(i)
                if head and LOCAL:
                    queries_out(i, ready, 0)
                if pre:
                    act.wait_ge(s.pre_t, i + 2)
                    if SELF:
                        at_least(act, s.kT, i)
                    if LOCAL:
                        copy(xsT_tokens[0:64, 1 - par, :, :], b[5][0:64, 0:128].rearrange("p (a q) -> p a q", q=SEQ))\
                            .then_inc(s.pre_copied, 1)
                        copy(xsT_tokens[64:128, 1 - par, :, 1:SEQ],
                             b[5][64:128, 0:128].rearrange("p (a q) -> p a q", q=SEQ)[:, :, 0:SEQ - 1])\
                            .then_inc(s.pre_copied, 1)
                    else:
                        copy(xsT[1 - par], b[5][:, 0:128]).then_inc(s.pre_copied, 1)
                    if CROSS:
                        copy(m.ctxT[:, 1 - par, :], b[5][:, 128:256]).then_inc(s.pre_copied, 1)
                if head and CROSS:
                    queries_out(i, ready, 0)
                if head and not late:
                    values_out(i, par, 0)
                if head and CROSS:
                    values_out(i, par, 1)
                    queries_out(i, ready, 1)
                    keys_out(i, ready, 0)
                    keys_out(i, ready, 1)
                if head and LOCAL:
                    queries_out(i, ready, 1)
                    keys_out(i, ready, 0)
                if tail and LOCAL:
                    act.wait_ge(s.sh, i - 1)
                    at_least(act, s.xn, i - 2)
                    copy(m.ys[:, 64:128], b[4][:, 128:192]).then_inc(s.sh_copied, 1)
                if head and late:
                    values_out(i, par, 0)
                if mid and not LOCAL:
                    probs_out(i - 1, 0)
                    probs_out(i - 1, 1)

            run_pipeline(act, turn, N)

        @block.vector
        def _(dve):
            tt = nc.vector.tensor_tensor

            def chunk(buf, j):
                return buf[:, j * 512:(j + 1) * 512].rearrange("p (h d) -> p h d", d=HD)

            def squares_summed(i, j):
                dve.wait_ge(s.sq, 4 * i + j + 1)
                nc.vector.tensor_reduce(m.ss[:, 8 * j:8 * j + 8], chunk(m.sq, j), AX.X, ALU.add).then_inc(s.ss, 1)

            def cosine_part(i, j):
                dve.wait_ge(s.qk, 4 * i + j + 1)
                at_least(dve, s.rotated, 4 * (i - 1) + j + 1)
                tab = m.tables[:, bass.ds(i // TILES, 1), j // 2, 0, :].to_broadcast([128, 8, HD])
                tt(chunk(m.RA, j), b[j][:, :].rearrange("p (h d) -> p h d", d=HD), tab, ALU.mult).then_inc(s.ra, 1)

            def sine_part(i, j):
                half = HD // 2
                dve.wait_ge(s.qk, 4 * i + j + 1)
                at_least(dve, s.qn, 4 * (i - 1) + j + 1)
                src, dst = b[j][:, :].rearrange("p (h d) -> p h d", d=HD), chunk(m.RB, j)
                for to, frm in ((0, half), (half, 0)):
                    tab = m.tables[:, bass.ds(i // TILES, 1), j // 2, 1, to:to + half].to_broadcast([128, 8, half])
                    last = tt(dst[:, :, to:to + half], src[:, :, frm:frm + half], tab, ALU.mult)
                last.then_inc(s.half, 1)

            def over_length(i, j):
                dve.wait_ge(s.newton, NRN * (i + 1))
                dve.wait_ge(s.rotated, 4 * i + j + 1)
                at_least(dve, s.rot, 4 * (i - 1) + j + 1)
                tt(chunk(m.qn, j), chunk(m.RB, j), m.rn[:, 8 * j:8 * j + 8].unsqueeze(2).to_broadcast([128, 8, HD]),
                   ALU.mult).then_inc(s.qn, 1)

            def less_maximum(i, j):
                at_least(dve, s.diff, 2 * (i - 2) + j + 1)
                dve.wait_ge(s.scores, 2 * (i - 1) + j + 1)
                rows = b[4 + j][:, :].rearrange("p (n k) -> p n k", k=SEQ)
                nc.vector.tensor_reduce(m.mx[:, 8 * j:8 * j + 8], rows, AX.X, ALU.max).then_inc(s.mx, 1)
                dve.wait_ge(s.mx, 2 * (i - 1) + j + 1)
                tt(m.D[:, j * 512:(j + 1) * 512].rearrange("p (n k) -> p n k", k=SEQ), rows,
                   m.mx[:, 8 * j:8 * j + 8].unsqueeze(2).to_broadcast([128, 8, SEQ]), ALU.subtract)\
                    .then_inc(s.diff, 1)

            def row_sums(i, j):
                heads = slice(8 * j, 8 * j + 8)
                at_least(dve, s.recip, 2 * (i - 2) + j + 1)
                dve.wait_ge(s.probs, 2 * (i - 1) + j + 1)
                nc.vector.tensor_reduce(m.row_sum[:, heads], m.P[:, j * 512:(j + 1) * 512].rearrange("p (n k) -> p n k", k=SEQ),
                                        AX.X, ALU.add).then_inc(s.row_sum, 1)
                at_least(dve, s.pnorm, 2 * (i - 2) + j + 1)
                dve.wait_ge(s.row_sum, 2 * (i - 1) + j + 1)
                nc.vector.reciprocal(m.inv_sum[:, heads], m.row_sum[:, heads]).then_inc(s.recip, 1)

            def gated(t, c):
                rows = FF_CHUNKS[c][1]
                dve.wait_ge(s.gelu, 3 * ((t - 1) // 2) + c + 1)
                nc.vector.scalar_tensor_tensor(
                    out=m.H[0:rows, c, :], in0=b[FF_BANKS[c]][0:rows, 256:512],
                    scalar=m.b1col[0:rows, 0, c, bass.ds(t // TILES, 1)],
                    in1=m.G[0:rows, c, :], op0=ALU.add, op1=ALU.mult).then_inc(s.h, 1)

            def statistics(i, row):
                at_least(dve, s.xn, i - 2)
                if LOCAL:
                    dve.wait_ge(s.sh_copied, i - 1)
                    dve.wait_ge(s.ys, i - 1)
                else:
                    dve.wait_ge(s.y1, i - 1)
                hold(dve, held)
                nc.vector.bn_stats(m.stats[:, :], row).then_inc(s.stats, 1)
                dve.wait_ge(s.stats, i - 1)
                hold(dve, held)
                nc.vector.bn_aggr(m.mv[:, :], m.stats[:, :]).then_inc(s.var, 1)

            def normalised(i, row):
                dve.wait_ge(s.rstd, i - 1)
                nc.vector.tensor_scalar(m.xn[:, :] if LOCAL else tile_of(m.Y, i - 2), row, m.mv[:, 0:1], m.rstd[:, 0:1],
                                        ALU.subtract, ALU.mult).then_inc(s.xn, 1)

            def turn(i, par, pre, head, mid, tail):
                late = LOCAL and trails(i, par, pair=True)
                rotary = head and LOCAL
                if rotary:
                    at_least(dve, s.seed, 3 * i)
                    squares_summed(i, 0)
                    cosine_part(i, 0)
                if LOCAL and trails(i, par):
                    statistics(i - 1, m.ys[:, :])
                if rotary:
                    squares_summed(i, 1)
                    sine_part(i, 0)
                    squares_summed(i, 2)
                if LOCAL and trails(i, par):
                    normalised(i - 1, m.ys[:, :])
                if rotary:
                    squares_summed(i, 3)
                    dve.wait_ge(s.ss, 4 * (i + 1))
                    at_least(dve, s.newton, NRN * i)
                    nc.vector.tensor_scalar(m.ssm[:, :], m.ss[:, :], 1e-24, None, ALU.max).then_inc(s.seed, 1)
                    dve.wait_ge(s.seed, 3 * i + 1)
                    nc.vector.tensor_scalar(m.bits[:, :], m.ssm[:, :].bitcast(I32), 1, None, ALU.arith_shift_right)\
                        .then_inc(s.seed, 1)
                    dve.wait_ge(s.seed, 3 * i + 2)
                    nc.vector.tensor_scalar(m.seed[:, :], m.bits[:, :], -1.0, RSQRT_MAGIC, ALU.mult, ALU.add)\
                        .then_inc(s.seed, 1)
                if rotary:
                    cosine_part(i, 1)
                if late:
                    gated(i - 3, 0)
                if rotary:
                    sine_part(i, 1)
                if late:
                    gated(i - 3, 1)
                if rotary:
                    cosine_part(i, 2)
                if late:
                    gated(i - 3, 2)
                if mid:
                    less_maximum(i, 0)
                if rotary:
                    sine_part(i, 2)
                if rotary and late:
                    cosine_part(i, 3)
                    over_length(i, 0)
                if late:
                    dve.wait_ge(s.w2, (i - 4) // 2 + 1)
                    pairs = m.Y[:, :, :].rearrange("p (t a) d -> p t (a d)", a=2)
                    tt(flat(pairs[:, bass.ds((i - 4) // 2 % (TILES // 2), 1), :]), flat(m.y1[:, :, :]), b[7][:, 0:256],
                       ALU.add).then_inc(s.y, 1)
                if mid:
                    less_maximum(i, 1)
                if rotary and not late:
                    over_length(i, 0)
                    cosine_part(i, 3)
                if rotary:
                    sine_part(i, 3)
                if head and SELF:
                    dve.wait_ge(s.qk, i + 1)
                    at_least(dve, s.scores, 2 * i)
                    for bb in range(2):
                        tt(qTbd[:, :, bb, :, :],
                           b[0][:, bb * 64:(bb + 1) * 64].unsqueeze(1).unsqueeze(1).to_broadcast([128, PAIRS, 2, SEQ]),
                           m.heads8[:, :].rearrange("p (a c) -> p a c", c=2).unsqueeze(3).to_broadcast([128, PAIRS, 2, SEQ]),
                           ALU.mult).then_inc(s.qT, 1)
                if mid:
                    row_sums(i, 0)
                if rotary:
                    over_length(i, 1)
                if mid:
                    row_sums(i, 1)
                if rotary:
                    over_length(i, 2)
                if tail:
                    if LOCAL:
                        dve.wait_ge(s.y, TILES // 2 + (i - 2) // 2)
                    dve.wait_ge(s.wo, i - 1)
                    src = tile_of(m.Y if LOCAL else m.X, i - 2)
                    dst = m.y1[:, par, :] if LOCAL else src
                    tt(dst, src, b[4][:, 0:128], ALU.add).then_inc(s.y1, 1)
                    if LOCAL:
                        at_least(dve, s.xn, i - 2)
                        tt(m.ys[:, 0:64], src[:, 0:64], b[4][:, 0:64], ALU.add).then_inc(s.ys, 1)
                if rotary:
                    over_length(i, 3)
                if tail and not LOCAL:
                    statistics(i, tile_of(m.X, i - 2))
                    normalised(i, tile_of(m.X, i - 2))

            if LOCAL:
                dve.sem_inc(s.y, TILES // 2)
            run_pipeline(dve, turn, N)

        @block.gpsimd
        def _(pool):
            tt = nc.gpsimd.tensor_tensor

            def inverse_deviation(i):
                at_least(pool, s.rstd, i - 2)
                pool.wait_ge(s.var, i - 1)
                hold(pool, held)
                nc.gpsimd.tensor_scalar(m.vare[:, :], m.mv[:, 1:2], EPS, None, ALU.add).then_inc(s.vare, 1)
                pool.wait_ge(s.vare, i - 1)
                tt(m.rstd[:, :], m.vare[:, :], m.minus_half[:, :], ALU.pow).then_inc(s.rstd, 1)

            def inverse_lengths(i):
                pool.wait_ge(s.seed, 3 * (i + 1))
                at_least(pool, s.newton, NRN * i)
                at_least(pool, s.qn, 4 * i)
                y = m.seed[:, :].bitcast(FP32)
                for step in range(3):
                    done = NRN * i + 4 * step
                    if step:
                        pool.wait_ge(s.newton, done)
                    tt(m.rn_a[:, :], y, y, ALU.mult).then_inc(s.newton, 1)
                    pool.wait_ge(s.newton, done + 1)
                    tt(m.rn_b[:, :], m.rn_a[:, :], m.ssm[:, :], ALU.mult).then_inc(s.newton, 1)
                    pool.wait_ge(s.newton, done + 2)
                    hold(pool, held)
                    nc.gpsimd.tensor_scalar(m.rn_a[:, :], m.rn_b[:, :], -0.5, 1.5, ALU.mult, ALU.add)\
                        .then_inc(s.newton, 1)
                    pool.wait_ge(s.newton, done + 3)
                    tt(m.rn[:, :], y, m.rn_a[:, :], ALU.mult).then_inc(s.newton, 1)
                    y = m.rn[:, :]

            def rotary_sum(i, j):
                at = slice(j * 512, (j + 1) * 512)
                pool.wait_ge(s.half, 4 * i + j + 1)
                pool.wait_ge(s.ra, 4 * i + j + 1)
                tt(m.RB[:, at], m.RB[:, at], m.RA[:, at], ALU.add).then_inc(s.rotated, 1)

            def normalised_probs(i, j):
                pool.wait_ge(s.recip, 2 * (i - 1) + j + 1)
                probs = m.P[:, j * 512:(j + 1) * 512].rearrange("p (n k) -> p n k", k=SEQ)
                tt(probs, probs, m.inv_sum[:, 8 * j:8 * j + 8].unsqueeze(2).to_broadcast([128, 8, SEQ]), ALU.mult)\
                    .then_inc(s.pnorm, 1)

            def turn(i, par, pre, head, mid, tail):
                if pre:
                    if LOCAL:
                        pool.wait_ge(s.y, (i + 1) // 2 + 1)
                    at_least(pool, s.pre_t, i + 1)
                    hold(pool, held)
                    nc.gpsimd.tensor_copy(m.ystat[:, :], tile_of(m.Y, i + 1)).then_inc(s.ystat, 1)
                if head and CROSS:
                    at_least(pool, s.scores, 2 * (i - 1))
                    hold(pool, held)
                    row = m.maskb[:, bass.ds(i * 128, 128)]
                    nc.gpsimd.tensor_copy(m.maskrow[:, par, :, :], row.unsqueeze(1).to_broadcast([1, 4, 128]))\
                        .then_inc(s.mask_made, 1)
                if LOCAL and trails(i, par):
                    inverse_deviation(i - 1)
                if head and LOCAL:
                    rotary_sum(i, 0)
                    inverse_lengths(i)
                    for j in range(1, 4):
                        rotary_sum(i, j)
                if mid:
                    normalised_probs(i, 0)
                    normalised_probs(i, 1)
                if tail and not LOCAL:
                    inverse_deviation(i)

            run_pipeline(pool, turn, N)


def constants():
    f32 = np.float32
    c = {}
    c["c_ident"] = np.eye(128, dtype=f32)
    t = np.arange(128)
    c["c_shift"] = ((t[None, :] == t[:, None] + 1) & (t[None, :] % SEQ != 0)).astype(f32)
    q, k = t[:, None] % SEQ, np.arange(512)[None, :] % SEQ
    c["c_causal"] = np.where((k > q) | (q > k + WINDOW), f32(MASKED), f32(0))
    half = np.arange(0, HD, 2, dtype=f32)
    inv_freq = (1.0 / np.power(f32(10000.0), half / f32(HD))).astype(f32)
    pos = np.arange(SEQ, dtype=f32)
    freqs = np.tile(pos[:, None] * inv_freq[None, :], (1, 2)).astype(f32)
    base = ((half + f32(0.4 * HD)) / f32(1.4 * HD)).astype(f32)
    power = ((pos - SEQ // 2) / (WINDOW // 2)).astype(f32)
    scale = np.tile(np.power(base[None, :], power[:, None]), (1, 2)).astype(f32)
    cos, sin = np.cos(freqs), np.sin(freqs)
    sin[:, :HD // 2] *= -1
    rot = np.stack([np.stack([cos * scale, sin * scale], 1), np.stack([cos / scale, sin / scale], 1)], 1)
    c["c_rot"] = np.ascontiguousarray(np.tile(rot, (2, 1, 1, 1)), dtype=f32)
    c["c_heads8"] = (t[:, None] // SD == np.arange(HEADS)[None, :]).astype(f32)
    return c


def kernel(**inputs):
    import concourse.bacc as bacc
    from concourse.bass_utils import run_bass_kernel_spmd as run

    a = {k: np.asarray(v) for k, v in inputs.items()}
    arrays = dict(
        x=a["x"], ctx_in=a["ctx_1024"], mask=a["mask_BxS2_bk0"].reshape(1, -1).view(np.int32),
        params=a["L0_attn_params"], wvT=a["L0_attn_Wv"].T, bv=a["L0_attn_bv"].reshape(1, -1),
        woT_a=a["L0_attn_Wo"].T, bo=a["L0_attn_bo"].reshape(1, -1),
        wq=a["L0_xattn_W_Q"], wk=a["L0_xattn_W_K"], wv=a["L0_xattn_W_V"], wo_x=a["L0_xattn_W_O"],
        wqkv=a["L0_ffn_Wqkv"], q_scale=a["L0_ffn_q_scale"], k_scale=a["L0_ffn_k_scale"], wo=a["L0_ffn_Wo"],
        ln_gT=a["L0_ffn_ln_g"].T, ln_bT=a["L0_ffn_ln_b"].T, w1=a["L0_ffn_W1"], b1T=a["L0_ffn_b1"].T,
        w2=a["L0_ffn_W2"], b2=a["L0_ffn_b2"], **constants())
    nc = bacc.Bacc("TRN2", target_bir_lowering=False, num_devices=1)
    feeds, aps = {}, []
    for name, v in arrays.items():
        v = np.ascontiguousarray(v)
        feeds["in_" + name] = v
        aps.append(nc.dram_tensor("in_" + name, v.shape, mybir.dt.from_np(v.dtype), kind="ExternalInput").ap())
    aps.append(nc.dram_tensor("out_0", (BATCH, SEQ, DIM), FP32, kind="ExternalOutput").ap())
    build(nc, *aps)
    r = run(nc, [feeds], core_ids=[0])
    return r.results[0]["out_0"]
```
